# Optimizing a Trainium2 kernel written in Bass

```python
import numpy as np
import jax
import jax.numpy as jnp

def _softmax(x, axis=-1):
    return jax.nn.softmax(x, axis=axis)
def _gelu(x):
    return jax.nn.gelu(x, approximate=True)
def _silu(x):
    return jax.nn.silu(x)
def _sigmoid(x):
    return jax.nn.sigmoid(x)
def _layernorm(x, axis=-1, eps=1e-5):
    m = jnp.mean(x, axis=axis, keepdims=True)
    v = jnp.var(x, axis=axis, keepdims=True)
    return (x - m) / jnp.sqrt(v + eps)
def _scatter_add(tgt, idx, src, axis=0):
    return tgt.at[idx].add(src)
def _segment_sum(src, seg, n):
    return jax.ops.segment_sum(src, seg, n)

kernel_name = 'mk_conv_preact_d2_conv_nhwc96_7dc06e'

def setup_inputs(seed: int = 0):
    np.random.seed(seed)
    _w = jnp.asarray
    def _rec_inputs():
        import jax
        import jax.numpy as jnp
        _gk = jax.random.key(seed)
        x = -0.0001476 + 0.9999 * jax.random.normal(jax.random.fold_in(_gk, 1), (32, 112, 112, 96), jnp.float32)
        return x
    x = _rec_inputs()
    def _L0_conv_setup():
        import jax, jax.numpy as jnp
        import numpy as np
        WS = 7
        SS = 3
        NH = 3

        def _rel_pos_index(ws):
            coords = np.stack(np.meshgrid(np.arange(ws), np.arange(ws), indexing='ij')).reshape(2, -1)
            rel = coords[:, :, None] - coords[:, None, :]
            rel = rel.transpose(1, 2, 0).copy()
            rel[..., 0] += ws - 1
            rel[..., 1] += ws - 1
            rel[..., 0] *= 2 * ws - 1
            return rel.sum(-1)

        def _attn_mask(H, W, ws, ss):
            img = np.zeros((H, W))
            cnt = 0
            slices = (slice(0, -ws), slice(-ws, -ss), slice(-ss, None))
            for h in slices:
                for w in slices:
                    img[h, w] = cnt
                    cnt += 1
            img = np.roll(img, (-ss, -ss), axis=(0, 1))
            mw = img.reshape(H // ws, ws, W // ws, ws).transpose(0, 2, 1, 3).reshape(-1, ws * ws)
            d = mw[:, None, :] - mw[:, :, None]
            return np.where(d != 0, -1000000000.0, 0.0).astype(np.float32)
        key = jax.random.key(seed)
        ks = jax.random.split(key, 6)
        B, H, W, C = (32, 112, 112, 96)
        return {'x': jax.random.normal(ks[0], (B, H, W, C), jnp.float32), 'qkv_w': jax.random.normal(ks[1], (C, 3 * C), jnp.float32) * 0.02, 'qkv_b': jax.random.normal(ks[2], (3 * C,), jnp.float32) * 0.02, 'proj_w': jax.random.normal(ks[3], (C, C), jnp.float32) * 0.02, 'proj_b': jax.random.normal(ks[4], (C,), jnp.float32) * 0.02, 'bias_table': jax.random.normal(ks[5], ((2 * WS - 1) ** 2, NH), jnp.float32) * 0.02}
    _L0_conv_all = _L0_conv_setup()
    _L0_conv_in = {k: v for k, v in _L0_conv_all.items() if k in ('qkv_w', 'qkv_b', 'proj_w', 'proj_b', 'bias_table', )}
    del _L0_conv_all

    def _L1_conv_setup():
        import jax, jax.numpy as jnp
        from jax import lax
        import numpy as np
        B, H, W, CH, N = (32, 112, 112, 96, 5)
        key = jax.random.key(seed)
        k1, k2 = jax.random.split(key)
        x = jax.random.normal(k1, (B, H, W, CH), dtype=jnp.float32)
        kernel = jax.random.normal(k2, (N, N, CH), dtype=jnp.float32)
        alpha = jnp.ones((1, 1), dtype=jnp.float32)
        bias = jnp.ones((1, 1), dtype=jnp.float32)
        return {'x': x, 'kernel': kernel, 'alpha': alpha, 'bias': bias}
    _L1_conv_all = _L1_conv_setup()
    _L1_conv_in = {k: v for k, v in _L1_conv_all.items() if k in ('kernel', 'alpha', 'bias', )}
    del _L1_conv_all

    return {
        "x": x,
        "L0_conv_qkv_w": _L0_conv_in["qkv_w"],
        "L0_conv_qkv_b": _L0_conv_in["qkv_b"],
        "L0_conv_proj_w": _L0_conv_in["proj_w"],
        "L0_conv_proj_b": _L0_conv_in["proj_b"],
        "L0_conv_bias_table": _L0_conv_in["bias_table"],
        "L1_conv_kernel": _L1_conv_in["kernel"],
        "L1_conv_alpha": _L1_conv_in["alpha"],
        "L1_conv_bias": _L1_conv_in["bias"],
    }

def reference(x, L0_conv_qkv_w, L0_conv_qkv_b, L0_conv_proj_w, L0_conv_proj_b, L0_conv_bias_table, L1_conv_kernel, L1_conv_alpha, L1_conv_bias):
    import jax
    import jax.numpy as jnp
    def _L0_conv_ref(x, qkv_w, qkv_b, proj_w, proj_b, bias_table):
        import jax, jax.numpy as jnp
        import numpy as np
        WS = 7
        SS = 3
        NH = 3

        def _rel_pos_index(ws):
            coords = np.stack(np.meshgrid(np.arange(ws), np.arange(ws), indexing='ij')).reshape(2, -1)
            rel = coords[:, :, None] - coords[:, None, :]
            rel = rel.transpose(1, 2, 0).copy()
            rel[..., 0] += ws - 1
            rel[..., 1] += ws - 1
            rel[..., 0] *= 2 * ws - 1
            return rel.sum(-1)

        def _attn_mask(H, W, ws, ss):
            img = np.zeros((H, W))
            cnt = 0
            slices = (slice(0, -ws), slice(-ws, -ss), slice(-ss, None))
            for h in slices:
                for w in slices:
                    img[h, w] = cnt
                    cnt += 1
            img = np.roll(img, (-ss, -ss), axis=(0, 1))
            mw = img.reshape(H // ws, ws, W // ws, ws).transpose(0, 2, 1, 3).reshape(-1, ws * ws)
            d = mw[:, None, :] - mw[:, :, None]
            return np.where(d != 0, -1000000000.0, 0.0).astype(np.float32)
        B, H, W, C = x.shape
        ws, ss, nh = (WS, SS, NH)
        hd = C // nh
        scale = hd ** (-0.5)
        N = ws * ws
        x = jnp.roll(x, (-ss, -ss), axis=(1, 2))
        xw = x.reshape(B, H // ws, ws, W // ws, ws, C).transpose(0, 1, 3, 2, 4, 5).reshape(-1, N, C)
        BnW = xw.shape[0]
        qkv = (xw @ qkv_w + qkv_b).reshape(BnW, N, 3, nh, hd).transpose(2, 0, 3, 1, 4)
        q, k, v = (qkv[0] * scale, qkv[1], qkv[2])
        attn = jnp.einsum('bhnd,bhmd->bhnm', q, k)
        rel_idx = jnp.asarray(_rel_pos_index(ws))
        bias = bias_table[rel_idx.reshape(-1)].reshape(N, N, nh).transpose(2, 0, 1)
        attn = attn + bias[None]
        mask = jnp.asarray(_attn_mask(H, W, ws, ss))
        nW = mask.shape[0]
        attn = (attn.reshape(-1, nW, nh, N, N) + mask[None, :, None]).reshape(BnW, nh, N, N)
        attn = jax.nn.softmax(attn, axis=-1)
        out = jnp.einsum('bhnm,bhmd->bhnd', attn, v).transpose(0, 2, 1, 3).reshape(BnW, N, C)
        out = out @ proj_w + proj_b
        xo = out.reshape(B, H // ws, W // ws, ws, ws, C).transpose(0, 1, 3, 2, 4, 5).reshape(B, H, W, C)
        return jnp.roll(xo, (ss, ss), axis=(1, 2))

    def _L1_conv_ref(x, kernel, alpha, bias):
        import jax, jax.numpy as jnp
        from jax import lax
        import numpy as np
        B, H, W, CH, N = (32, 112, 112, 96, 5)
        ch = x.shape[-1]
        rhs = kernel[:, :, None, :]
        conv = lax.conv_general_dilated(x, rhs, window_strides=(1, 1), padding='SAME', dimension_numbers=('NHWC', 'HWIO', 'NHWC'), feature_group_count=ch)
        gate = conv * alpha[0, 0] + bias[0, 0]
        return gate * x + x

    def _gn(v, G=32, eps=1e-5):
        B_, H_, W_, C_ = v.shape
        g = v.reshape(B_, H_, W_, G, C_ // G)
        m = jnp.mean(g, axis=(1, 2, 4), keepdims=True)
        s = jnp.var(g, axis=(1, 2, 4), keepdims=True)
        return ((g - m) / jnp.sqrt(s + eps)).reshape(v.shape)

    def _ln_c(v, eps=1e-6):
        m = jnp.mean(v, axis=-1, keepdims=True)
        s = jnp.var(v, axis=-1, keepdims=True)
        return (v - m) / jnp.sqrt(s + eps)

    def _ln_t(v, eps=1e-5):
        m = jnp.mean(v, axis=-1, keepdims=True)
        s = jnp.var(v, axis=-1, keepdims=True)
        return (v - m) / jnp.sqrt(s + eps)

    def _to_tokens(v):
        B_, H_, W_, C_ = v.shape
        return v.reshape(B_, H_ * W_, C_)
    def _from_tokens(t, like):
        return t.reshape(like.shape)

    x = x + _L0_conv_ref(_gn(x), L0_conv_qkv_w, L0_conv_qkv_b, L0_conv_proj_w, L0_conv_proj_b, L0_conv_bias_table)
    x = x + _L1_conv_ref(_gn(x), L1_conv_kernel, L1_conv_alpha, L1_conv_bias)
    return x


_drawn_inputs = setup_inputs


def setup_inputs(seed=0):
    import zlib

    import numpy as np

    out = dict(_drawn_inputs(seed))
    spreads = {}
    factors = {'L0_conv_qkv_w': 6.798,
     'L0_conv_qkv_b': 8.0,
     'L0_conv_proj_w': 6.266,
     'L0_conv_proj_b': 3.01,
     'L0_conv_bias_table': 8.0}
    for name, (base, spread) in spreads.items():
        noise = np.random.default_rng([zlib.crc32(name.encode()), seed]).standard_normal(out[name].shape)
        drawn = base * np.exp(spread * noise) if base else spread * noise
        out[name] = jnp.asarray(drawn.astype(out[name].dtype))
    for name, factor in factors.items():
        out[name] = (out[name] * factor).astype(out[name].dtype)
    return out
```

```python
from contextlib import ExitStack

import concourse.bass as bass
from concourse import mybir

F32 = mybir.dt.float32
ALU = mybir.AluOpType
ACT = mybir.ActivationFunctionType
AX_X = mybir.AxisListType.X

NI, H, W, C = 32, 112, 112, 96
WS, SS, NH = 7, 3, 3
HD = C // NH
NW = H // WS
TOK = WS * WS
PAD = 64
PAIRP = PAD + TOK
STRIP = NW * TOK
NP = NW // 2
PB = 512 // (NH * TOK)
CHUNKS = [(p, min(p + PB, NP)) for p in range(0, NP, PB)]
NCH = len(CHUNKS)
HP = NP // 2
HS = STRIP // 2
HV = HD + 1
SCALE = float(HD) ** -0.5
EPS = 1e-5
KS = 5
HALO = KS // 2
N_BAND = KS * KS * 4
PR, PC = 4, 32
OC = PC - KS + 1
NB, NWB = H // PR, W // OC
HB, WP = H + KS - 1, W + KS - 1
BLK = (NB + 1) * NWB
OUTB = NB * NWB
CG = 4
NCG = C // CG
ROWS = 3 * C
ROW_CUTS = [(0, SS, 96), (96, SS + 96, H - SS - 96), (H - SS, 0, SS)]


def attention_then_conv(nc, x, qkv_w, qkv_b, proj_w, proj_b, bias_win, taps, alpha, bias, masks, eye, group, out):
    y_pad = nc.dram_tensor("y_pad", (NI + 1, HB, WP, C), F32, kind="Internal").ap()
    rows_dram = nc.dram_tensor("rows_dram", (NI + 1, 128, ROWS), F32, kind="Internal").ap()
    band_dram = nc.dram_tensor("band_dram", (2, 128, 128, C), F32, kind="Internal").ap()

    ctx = ExitStack()
    with ctx:
        def sb(name, shape, space=ctx):
            return space.enter_context(nc.sbuf_tensor(name, shape, F32))

        def sem(name):
            return ctx.enter_context(nc.semaphore(name))

        ps_scores = ctx.enter_context(nc.psum_tensor("ps_scores", [128, NCH, 512], F32))
        bank3 = ctx.enter_context(nc.psum_tensor("bank34", [128, 2, 512], F32))
        bank = {b: ctx.enter_context(nc.psum_tensor(f"bank{b}", [128, 512], F32)) for b in (5, 6, 7)}

        def bk(b):
            return bank3[:, b - 3, :] if b < 5 else bank[b][:, :]

        ident = sb("ident", [128, 128])
        small = sb("small", [128, 16])
        alpha_col, gate_one = small[:, 0:1], small[:, 1:2]

        consts_in, consts_ready, zeros_ready, psum_ready = sem("consts_in"), sem("consts_ready"), sem("zeros_ready"), sem("psum_ready")
        setup_mm, setup_dve, setup_pool = sem("setup_mm"), sem("setup_dve"), sem("setup_pool")
        band_zeroed, band_written = sem("band_zeroed"), sem("band_written")
        xin_loaded, xres_loaded, y_stored = sem("xin_loaded"), sem("xres_loaded"), sem("y_stored")
        xT_done, xT_evac, x_stats = sem("xT_done"), sem("xT_evac"), sem("x_stats")
        xn_done, qk_done, q_evac, k_evac_act, k_evac_dve = (
            sem("xn_done"), sem("qk_done"), sem("q_evac"), sem("k_evac_act"), sem("k_evac_dve"))
        v_done, v_evac_act, v_evac_dve = sem("v_done"), sem("v_evac_act"), sem("v_evac_dve")
        scores_done, bias_added, max_done, sub_done, exp_done = (
            sem("scores_done"), sem("bias_added"), sem("max_done"), sem("sub_done"), sem("exp_done"))
        pt_done, pt_evac, av_done, recip_done, on_done = (
            sem("pt_done"), sem("pt_evac"), sem("av_done"), sem("recip_done"), sem("on_done"))
        ot_done, ot_evac, proj_done, y_done, yT_done, y_stats = (
            sem("ot_done"), sem("ot_evac"), sem("proj_done"), sem("y_done"), sem("yT_done"), sem("y_stats"))
        agg_dve, agg_pe, agg_pool, norm_ready, bc_ready = (
            sem("agg_dve"), sem("agg_pe"), sem("agg_pool"), sem("norm_ready"), sem("bc_ready"))
        agg_copy = sem("agg_copy")
        rows_mm, rows_evac, rows_stored = sem("rows_mm"), sem("rows_evac"), sem("rows_stored")
        band_in, band_copied = [sem("band_in0"), sem("band_in1")], [sem("band_copied0"), sem("band_copied1")]
        y_in = [sem("y_in0"), sem("y_in1")]
        z_ready, conv_done, gated, added_dve, added_pool, out_stored = (
            sem("z_ready"), sem("conv_done"), sem("gated"), sem("added_dve"), sem("added_pool"), sem("out_stored"))

        phase_b = ExitStack()
        with phase_b:
            def sbb(name, shape):
                return sb(name, shape, phase_b)

            xT = sbb("xT", [C, NW, NW, WS, WS])
            xin = sbb("xin", [H, WS, C])
            xres = sbb("xres", [H, WS, C])
            y_strip = sbb("y_strip", [H, WS, C])
            xn = sbb("xn", [C, NW, PAD])
            q_sb = sbb("q_sb", [C, STRIP])
            k_sb = sbb("k_sb", [C, NW, NH, TOK])
            v01 = sbb("v01", [128, NW, 2 * HV])
            v2 = sbb("v2", [128, HP, 2, 2, HV])
            t_sb = sbb("t_sb", [128, NP, NH, TOK])
            mx = sbb("mx", [128, NP, NH])
            p01 = sbb("p01", [128, NP, 2, PAD])
            p2 = sbb("p2", [128, NP, PAD])
            pt01 = sbb("pt01", [128, HP, 2, TOK])
            pt2 = sbb("pt2", [128, HP // 2, 2, TOK])
            rc = [sbb(f"rc{m}", [128, HP, NH]) for m in range(2)]
            o_norm = [sbb(f"o_norm{m}", [128, HP, NH, HD]) for m in range(2)]
            oT = sbb("oT", [C + 1, WS, NW, WS])
            bias_sb = sbb("bias_sb", [128, 3, NP, NH, TOK])
            bias_base = sbb("bias_base", [128, NH, TOK])
            mask_sb = sbb("mask_sb", [128, 3, 2, TOK])
            w_qkv = sbb("w_qkv", [C, 3 * C])
            w_proj = sbb("w_proj", [C + 1, C])
            b_qkv = sbb("b_qkv", [C, 3])
            b_proj = sbb("b_proj", [C + 1, C])
            group_sb = sbb("group_sb", [C, C])
            x_bn = sbb("x_bn", [C, NW, 2, 6])
            y_bn = sbb("y_bn", [C, NW, 2, 6])
            y_agg_in = sbb("y_agg_in", [C, NW, 2, 6])
            mv = sbb("mv", [C, 2, 2])
            dev = sbb("dev", [C, 2])
            spread = sbb("spread", [C, 2])
            var_eps = sbb("var_eps", [C, 2])
            carrier = sbb("carrier", [C, 1])
            minus_half = sbb("minus_half", [C, 2])
            stat = sbb("stat", [C, 3, 2])
            stat_bc = sbb("stat_bc", [C, 3, 128])
            rows_sb = sbb("rows_sb", [128, ROWS])
            zeros = sbb("zeros", [128, 16 * C])

            b_q_scaled = small[0:C, 2:3]
            def xin_count(n, j):
                return 16 * len(ROW_CUTS) * ((NW + 1) * n + j + 1) + (16 * len(ROW_CUTS) if isinstance(j, int) and j == NW - 1 else 0)

            ACT_KEYS, DVE_KEYS = (0, 1), (2,)

            def key_block(i, b, h):
                rows_ = slice(HD * h, HD * h + HD)
                return (rows_, bk(b)[rows_, 0:HS].rearrange("c (w k) -> c w k", k=TOK),
                        k_sb[rows_, NP * i:NP * i + NP, h, :])

            block = phase_b.enter_context(nc.Block())

            def walk(eng, step, apart=1):
                def tail(n, ahead):
                    for j in range(NW - apart, NW):
                        step(n, j, True, ahead)

                step(0, 0, False, True)
                step(0, 1, True, True)
                with eng.Fori(2, NW - apart) as j:
                    step(0, j, True, True)
                tail(0, True)
                with eng.Fori(1, NI - 1) as n:
                    step(n, 0, True, True)
                    with eng.Fori(1, NW - apart) as j:
                        step(n, j, True, True)
                    tail(n, True)
                step(NI - 1, 0, True, False)
                with eng.Fori(1, NW - apart) as j:
                    step(NI - 1, j, True, False)
                tail(NI - 1, False)

            @block.sync
            def _(sp):
                sp.dma_start(ident[:, :], eye).then_inc(consts_in, 16)
                sp.dma_start(w_qkv[:, :], qkv_w).then_inc(consts_in, 16)
                sp.dma_start(w_proj[0:C, :], proj_w).then_inc(consts_in, 16)
                sp.dma_start(b_qkv[:, :], qkv_b).then_inc(consts_in, 16)
                sp.dma_start(b_proj[C:C + 1, :], proj_b).then_inc(consts_in, 16)
                for lo in (0, PAD):
                    if lo == 0:
                        sp.wait_ge(zeros_ready, 1)
                    sp.dma_start(bias_base[lo:lo + TOK, :, :], bias_win).then_inc(consts_in, 16)
                sp.dma_start(mask_sb[0:PAIRP, :, :, :], masks).then_inc(consts_in, 16)
                sp.dma_start(group_sb[:, :], group).then_inc(consts_in, 16)
                sp.dma_start(alpha_col, alpha.broadcast_to([128, 1])).then_inc(consts_in, 16)
                sp.dma_start(gate_one, bias.broadcast_to([128, 1])).then_inc(consts_in, 16)

                def column_cuts(j):
                    if isinstance(j, int) and j == NW - 1:
                        return [(0, WS * j + SS, W - WS * j - SS), (W - WS * j - SS, 0, SS)]
                    return [(0, WS * j + SS, WS)]

                def load(dst, n, j, done):
                    for p0, r0, nr in ROW_CUTS:
                        for w0, c0, ncol in column_cuts(j):
                            sp.dma_start(dst[p0:p0 + nr, w0:w0 + ncol, :],
                                         x[bass.ds(n, 1), r0:r0 + nr, bass.ds(c0, ncol), :].rearrange("a r w c -> (a r) w c")
                                         ).then_inc(done, 16)

                def store(n, j):
                    for p0, r0, nr in ROW_CUTS:
                        for w0, c0, ncol in column_cuts(j):
                            sp.dma_start(y_pad[bass.ds(n + 1, 1), r0 + HALO:r0 + HALO + nr, bass.ds(c0 + HALO, ncol), :]
                                         .rearrange("a r w c -> (a r) w c"),
                                         y_strip[p0:p0 + nr, w0:w0 + ncol, :]).then_inc(y_stored, 16)

                def stage(n, j, prev, ahead):
                    t = n * NW + j
                    if ahead:
                        sp.wait_ge(xT_done, 2 * (t + NW))
                        load(xin, n + 1, j, xin_loaded)
                    if prev:
                        sp.wait_ge(y_done, 2 * t)
                        if isinstance(j, int) and j == 0:
                            store(n - 1, NW - 1)
                        else:
                            store(n, j - 1)
                    load(xres, n, j, xres_loaded)

                def save_rows(n):
                    sp.wait_ge(rows_evac, n + 1)
                    sp.dma_start(rows_dram[bass.ds(n, 1), :, :].rearrange("a p c -> (a p) c"), rows_sb[:, :]).then_inc(rows_stored, 16)
                    image = y_pad[bass.ds(n, 1), :, :, :]
                    for e in (0, 1, HB - 2, HB - 1):
                        sp.dma_start(image[:, e, :, :].rearrange("a w c -> (a w) c"), rows_sb[0:WP, 0:C]).then_inc(rows_stored, 16)
                        sp.dma_start(image[:, 2:HB - 2, e, :].rearrange("a r c -> (a r) c"), rows_sb[0:H, 0:C]).then_inc(rows_stored, 16)

                load(xin, 0, 0, xin_loaded)
                with sp.Fori(1, NW - 1) as j:
                    sp.wait_ge(xT_done, 2 * j)
                    load(xin, 0, j, xin_loaded)
                sp.wait_ge(xT_done, 2 * (NW - 1))
                load(xin, 0, NW - 1, xin_loaded)

                stage(0, 0, False, True)
                with sp.Fori(1, NW - 1) as j:
                    stage(0, j, True, True)
                stage(0, NW - 1, True, True)
                save_rows(0)
                with sp.Fori(1, NI - 1) as n:
                    stage(n, 0, True, True)
                    with sp.Fori(1, NW - 1) as j:
                        stage(n, j, True, True)
                    stage(n, NW - 1, True, True)
                    save_rows(n)
                stage(NI - 1, 0, True, False)
                with sp.Fori(1, NW - 1) as j:
                    stage(NI - 1, j, True, False)
                stage(NI - 1, NW - 1, True, False)
                save_rows(NI - 1)
                sp.wait_ge(y_done, 2 * NI * NW)
                store(NI - 1, NW - 1)
                save_rows(NI)
                sp.wait_ge(y_stored, xin_count(NI - 1, NW - 1))
                sp.wait_ge(rows_stored, 16 * 9 * (NI + 1))
                sp.wait_ge(band_written, 16 * N_BAND)

            @block.gpsimd
            def _(pool):
                nc.gpsimd.memset(zeros[:, :], 0.0).then_inc(setup_pool, 1)
                nc.gpsimd.memset(bias_base[:, :, :], 0.0).then_inc(zeros_ready, 1)
                nc.gpsimd.memset(xn[:, :, :], 0.0).then_inc(setup_pool, 1)
                nc.gpsimd.memset(v01[:, :, :], 0.0).then_inc(setup_pool, 1)
                nc.gpsimd.memset(k_sb[:, :, :, :], 0.0).then_inc(setup_pool, 1)
                nc.gpsimd.memset(v2[:, :, :, :, :], 0.0).then_inc(setup_pool, 1)
                nc.gpsimd.memset(p01[:, :, :, :], 0.0).then_inc(setup_pool, 1)
                nc.gpsimd.memset(p2[:, :, :], 0.0).then_inc(setup_pool, 1)
                nc.gpsimd.memset(y_bn[:, :, :, :], 1.0).then_inc(setup_pool, 1)
                nc.gpsimd.memset(y_agg_in[:, :, :, :], 1.0).then_inc(setup_pool, 1)
                nc.gpsimd.memset(minus_half[:, :], -0.5).then_inc(setup_pool, 1)
                pool.wait_ge(setup_pool, 10)
                nc.gpsimd.memset(oT[C:C + 1, :, :, :], 1.0).then_inc(setup_pool, 1)
                for i, lo in enumerate((0, PAD)):
                    pool.wait_ge(setup_pool, 11 + 2 * i)
                    nc.gpsimd.memset(v01[lo:lo + PAD, :, HV * i + HD:HV * i + HV], 1.0).then_inc(setup_pool, 1)
                    pool.wait_ge(setup_pool, 12 + 2 * i)
                    nc.gpsimd.memset(v2[lo:lo + PAD, :, :, i, HD:HV], 1.0).then_inc(setup_pool, 1)
                for half in range(2):
                    for g in range(128 // 16):
                        pool.dma_start(band_dram[half, :, 16 * g:16 * g + 16, :].rearrange("p m c -> p (m c)"),
                                       zeros[:, :]).then_inc(band_zeroed, 16)
                pool.wait_ge(band_zeroed, 16 * 16)
                for dy in range(KS):
                    for dx in range(KS):
                        for r in range(PR):
                            half, row = (r + dy) // PR, (r + dy) % PR
                            col = (r + KS // 2) % PR * PC + KS // 2
                            start = band_dram[half, row * PC + dx, col, 0:1]
                            diagonal = bass.AP(band_dram.tensor, start.offset, [[(128 + 1) * C, OC], [1, C]])
                            tap = taps[dy, dx:dx + 1, :].broadcast_to([OC, C])
                            pool.dma_start(diagonal, tap).then_inc(band_written, 16)

                def subtract(t, i):
                    p0, p1 = CHUNKS[i]
                    pool.wait_ge(max_done, NCH * t + i + 1)
                    nc.gpsimd.tensor_tensor(t_sb[0:PAIRP, p0:p1], t_sb[0:PAIRP, p0:p1],
                                            mx[0:PAIRP, p0:p1].unsqueeze(3).broadcast_to([PAIRP, p1 - p0, NH, TOK]),
                                            ALU.subtract).then_inc(sub_done, 1)

                def power(i):
                    pool.wait_ge(agg_dve, 3 * (i + 1))
                    nc.gpsimd.tensor_tensor(stat[:, 1, :], var_eps[:, :], minus_half[:, :], ALU.pow).then_inc(agg_pool, 1)

                power(0)

                def step(n, j, prev, ahead):
                    t = n * NW + j
                    for i in range(NCH):
                        subtract(t, i)
                    if isinstance(j, int) and j == NW - 1:
                        power(n + 1)

                walk(pool, step)
                power(NI + 1)

            @block.scalar
            def _(act):
                act.wait_ge(consts_ready, 2)
                act.wait_ge(setup_pool, 15)

                def evac_xT(s, slot):
                    for b, (w0, w1) in enumerate(((0, 4), (4, WS))):
                        act.wait_ge(xT_done, 2 * s + b + 1)
                        src = bk(3 + b)[0:C, 0:H * (w1 - w0)].rearrange("c (w i h) -> c w i h", i=NW, h=WS)
                        dst = xT[:, bass.ds(slot, 1), :, w0:w1, :].rearrange("c a i w h -> c w (a i) h")
                        nc.scalar.activation(dst, src, ACT.Copy).then_inc(xT_evac, 1)

                def normalise(t, slot, image):
                    act.wait_ge(norm_ready, image + 1)
                    act.wait_ge(xT_evac, 2 * (t + 1))
                    if not (isinstance(t, int) and t == 0):
                        act.wait_ge(v_done, t)
                    src = xT[:, bass.ds(slot, 1), :, :, :].rearrange("c a i w h -> c (a i) (w h)")
                    nc.scalar.activation(xn[:, :, 0:TOK], src, ACT.Identity, bias=stat[:, 2, 0:1],
                                         scale=stat[:, 1, 0:1]).then_inc(xn_done, 1)

                def evac_qk(t):
                    for i, b in enumerate((5, 6)):
                        act.wait_ge(qk_done, 4 * t + i + 1)
                        nc.scalar.activation(q_sb[:, HS * i:HS * i + HS], bk(b)[0:C, 0:HS], ACT.Identity,
                                             bias=b_q_scaled, scale=SCALE).then_inc(q_evac, 1)
                    for i, b in enumerate((3, 4)):
                        act.wait_ge(qk_done, 4 * t + i + 3)
                        for h in ACT_KEYS:
                            rows_, src, dst = key_block(i, b, h)
                            nc.scalar.activation(dst, src, ACT.Identity, bias=b_qkv[rows_, 1:2]).then_inc(k_evac_act, 1)

                def evac_oT(t, m, b):
                    act.wait_ge(ot_done, 2 * t + m + 1)
                    src = bk(b)[0:C, :].rearrange("c (i k) -> c i k", k=PAD)[:, :, 0:TOK].rearrange("c i (w h) -> c i w h", h=WS)
                    dst = oT[0:C, :, NP * m:NP * m + NP, :].rearrange("c w i h -> c i w h")
                    nc.scalar.activation(dst, src, ACT.Copy).then_inc(ot_evac, 1)

                def exps(t, i):
                    p0, p1 = CHUNKS[i]
                    act.wait_ge(sub_done, NCH * t + i + 1)
                    nc.scalar.activation(p01[0:PAIRP, p0:p1, :, 0:TOK], t_sb[0:PAIRP, p0:p1, 0:2], ACT.Exp).then_inc(exp_done, 1)
                    nc.scalar.activation(p2[0:PAIRP, p0:p1, 0:TOK], t_sb[0:PAIRP, p0:p1, 2], ACT.Exp).then_inc(exp_done, 1)

                def evac_pt(t, m):
                    for i, (b, dst, cnt) in enumerate(((5, pt01, HP), (6, pt2, HP // 2))):
                        act.wait_ge(pt_done, 4 * t + 2 * m + i + 1)
                        src = bk(b)[0:PAIRP, 0:128 * cnt].rearrange("k (p a q) -> k p a q", p=cnt, q=PAD)[:, :, :, 0:TOK]
                        nc.scalar.activation(dst[0:PAIRP, :, :, :], src, ACT.Copy).then_inc(pt_evac, 1)

                with act.Fori(0, NW) as j:
                    evac_xT(j, j)
                normalise(0, 0, 0)
                evac_qk(0)

                def step(n, j, prev, ahead):
                    t = n * NW + j
                    last = isinstance(j, int) and j == NW - 1
                    if prev:
                        evac_oT(t - 1, 1, 5)
                    act.wait_ge(v_done, t + 1)
                    src = bank3[0:TOK, :, 0:HP * C].rearrange("k b (p c) -> k b p c", c=C)
                    even = v01[:, :, :].rearrange("k (b p a) c -> k a b p c", b=2, a=2)
                    nc.scalar.activation(even[0:TOK, 0, :, :, 0:HD], src[:, :, :, 0:HD], ACT.Copy).then_inc(v_evac_act, 1)
                    nc.scalar.activation(even[PAD:PAIRP, 0, :, :, HV:HV + HD], src[:, :, :, HD:2 * HD], ACT.Copy).then_inc(v_evac_act, 1)
                    src2 = bank3[0:TOK, :, 0:HP * C].rearrange("k b (g o c) -> k o b g c", o=2, c=C)
                    dst2 = v2[:, :, :, :, :].rearrange("k (b g) a o c -> k a o b g c", b=2)
                    nc.scalar.activation(dst2[0:TOK, 0, 0, :, :, 0:HD], src2[:, 0, :, :, 2 * HD:C], ACT.Copy).then_inc(v_evac_act, 1)
                    nc.scalar.activation(dst2[PAD:PAIRP, 0, 1, :, :, 0:HD], src2[:, 1, :, :, 2 * HD:C], ACT.Copy).then_inc(v_evac_act, 1)
                    exps(t, 0)
                    if ahead:
                        evac_xT(t + NW, j)
                    exps(t, 1)
                    evac_pt(t, 0)
                    more = ahead or not last
                    if more:
                        normalise(t + 1, 0 if last else j + 1, n + 1 if last else n)
                    exps(t, 2)
                    if more:
                        evac_qk(t + 1)
                    evac_pt(t, 1)
                    evac_oT(t, 0, 7)
                    if last:
                        rows_out(n)

                def rows_out(n):
                    act.wait_ge(rows_mm, n + 1)
                    if not (isinstance(n, int) and n == 0):
                        act.wait_ge(rows_stored, 16 * 9 * n)
                    nc.scalar.activation(rows_sb[:, :], bk(4)[:, 0:ROWS], ACT.Copy).then_inc(rows_evac, 1)

                walk(act, step)
                evac_oT(NI * NW - 1, 1, 5)
                rows_out(NI)

            @block.vector
            def _(dve):
                for b in range(NCH):
                    nc.vector.memset(ps_scores[:, b, :], 1.0).then_inc(psum_ready, 1)
                for b in (3, 4, 5, 6, 7):
                    nc.vector.memset(bk(b), 1.0).then_inc(psum_ready, 1)
                dve.wait_ge(consts_in, 16 * 11)
                nc.vector.tensor_scalar(b_q_scaled, b_qkv[:, 0:1], SCALE, None, ALU.mult).then_inc(consts_ready, 1)
                nc.vector.tensor_scalar(gate_one, gate_one, 1.0, None, ALU.add).then_inc(setup_dve, 1)
                for k in range(3):
                    for p in range(NP):
                        nc.vector.tensor_tensor(bias_sb[0:PAIRP, k, p, :, :], bias_base[0:PAIRP, :, :],
                                                mask_sb[0:PAIRP, k, int(p == NP - 1), :].unsqueeze(1).broadcast_to([PAIRP, NH, TOK]),
                                                ALU.add).then_inc(setup_dve, 1)
                dve.wait_ge(setup_mm, 1)
                nc.vector.tensor_tensor(w_proj[C:C + 1, :], bk(7)[C:C + 1, 0:C], b_proj[C:C + 1, :], ALU.add).then_inc(consts_ready, 1)
                dve.wait_ge(setup_dve, 1 + 3 * NP)
                dve.wait_ge(setup_pool, 15)

                def x_statistics(s, slot):
                    dve.wait_ge(xT_evac, 2 * s + 2)
                    for b in range(2):
                        nc.vector.bn_stats(x_bn[:, bass.ds(slot, 1), b, :].rearrange("c a s -> c (a s)"),
                                           xT[:, bass.ds(slot, 1), NP * b:NP * b + NP, :, :].rearrange("c a i w h -> c (a i w h)")
                                           ).then_inc(x_stats, 1)

                def y_statistics(t, slot):
                    for b, wn in enumerate((4, WS - 4)):
                        dve.wait_ge(yT_done, 2 * t + b + 1)
                        nc.vector.bn_stats(y_bn[:, bass.ds(slot, 1), b, :].rearrange("c a s -> c (a s)"),
                                           bk(3 + b)[0:C, 0:H * wn]).then_inc(y_stats, 1)

                def aggregate(i, s, t, of_x):
                    if t is not None:
                        dve.wait_ge(y_stats, 2 * t)
                    nc.vector.tensor_copy(y_agg_in[:, NW - 1, :, :], y_bn[:, 0, :, :]).then_inc(agg_copy, 1)
                    if of_x:
                        dve.wait_ge(x_stats, 2 * s)
                        nc.vector.memset(carrier[:, :], 0.0)
                    nc.vector.bn_aggr(mv[:, 0, :], x_bn[:, :, :, :].rearrange("c a b s -> c (a b s)")).then_inc(agg_copy, 1)
                    dve.wait_ge(agg_copy, 7 * i + 2)
                    nc.vector.memset(carrier[:, :], 0.0)
                    nc.vector.bn_aggr(mv[:, 1, :], y_agg_in[:, :, :, :].rearrange("c a b s -> c (a b s)")).then_inc(agg_dve, 1)
                    dve.wait_ge(agg_dve, 3 * i + 1)
                    nc.vector.tensor_copy(y_agg_in[:, 0:NW - 1, :, :], y_bn[:, 1:NW, :, :]).then_inc(agg_copy, 1)
                    dve.wait_ge(agg_pe, 2 * i + 1)
                    nc.vector.tensor_copy(stat[:, 0, :], ps_scores[0:C, 0, 500:502]).then_inc(agg_copy, 1)
                    nc.vector.tensor_tensor(dev[:, :], mv[:, :, 0], ps_scores[0:C, 0, 500:502], ALU.subtract).then_inc(agg_copy, 1)
                    dve.wait_ge(agg_copy, 7 * i + 5)
                    nc.vector.tensor_tensor(spread[:, :], dev[:, :], dev[:, :], ALU.mult).then_inc(agg_copy, 1)
                    dve.wait_ge(agg_copy, 7 * i + 6)
                    nc.vector.tensor_tensor(spread[:, :], spread[:, :], mv[:, :, 1], ALU.add).then_inc(agg_dve, 1)
                    dve.wait_ge(agg_pe, 2 * i + 2)
                    nc.vector.tensor_scalar(var_eps[:, :], ps_scores[0:C, 0, 504:506], EPS, None, ALU.add).then_inc(agg_dve, 1)
                    dve.wait_ge(agg_pool, i + 1)
                    nc.vector.scalar_tensor_tensor(stat[:, 2, :], stat[:, 0, :], -1.0, stat[:, 1, :], ALU.mult, ALU.mult).then_inc(norm_ready, 1)
                    dve.wait_ge(norm_ready, i + 1)
                    nc.vector.tensor_copy(stat_bc[:, :, :], stat[:, :, 1:2].broadcast_to([C, 3, 128])).then_inc(agg_copy, 1)

                with dve.Fori(0, NW) as j:
                    x_statistics(j, j)
                aggregate(0, NW, None, True)

                def add_bias(t, i, kind):
                    p0, p1 = CHUNKS[i]
                    dve.wait_ge(scores_done, NCH * t + i + 1)
                    nc.vector.tensor_tensor(
                        t_sb[0:PAIRP, p0:p1].rearrange("q p h k -> q (p h k)"), ps_scores[0:PAIRP, i, 0:NH * TOK * (p1 - p0)],
                        bias_sb[0:PAIRP, kind, p0:p1].rearrange("q p h k -> q (p h k)"), ALU.add).then_inc(bias_added, 1)

                def row_max(t, i):
                    p0, p1 = CHUNKS[i]
                    dve.wait_ge(bias_added, NCH * t + i + 1)
                    nc.vector.tensor_reduce(mx[0:PAIRP, p0:p1], t_sb[0:PAIRP, p0:p1], AX_X, ALU.max).then_inc(max_done, 1)

                def move_keys(t):
                    for i, b in enumerate((3, 4)):
                        dve.wait_ge(qk_done, 4 * t + i + 3)
                        for h in DVE_KEYS:
                            rows_, src, dst = key_block(i, b, h)
                            nc.vector.tensor_scalar(dst, src, b_qkv[rows_, 1:2], None, ALU.add).then_inc(k_evac_dve, 1)

                def residual(t, last, this):
                    dve.wait_ge(xres_loaded, xin_count(*this))
                    if not (isinstance(t, int) and t == 0):
                        dve.wait_ge(y_stored, xin_count(*last))
                    for i, (b, w0, w1) in enumerate(((6, 0, 4), (7, 4, WS))):
                        dve.wait_ge(proj_done, 2 * t + i + 1)
                        nc.vector.tensor_tensor(y_strip[:, w0:w1, :].rearrange("h w c -> h (w c)"), bk(b)[0:H, 0:C * (w1 - w0)],
                                                xres[:, w0:w1, :].rearrange("h w c -> h (w c)"), ALU.add).then_inc(y_done, 1)

                def normalise_out(t, m, b):
                    dve.wait_ge(av_done, 2 * t + m + 1)
                    av = bk(b)[0:PAIRP, 0:HP * NH * HV].rearrange("q (p h d) -> q p h d", p=HP, d=HV)
                    nc.vector.reciprocal(rc[m][0:PAIRP], av[:, :, :, HD]).then_inc(recip_done, 1)
                    dve.wait_ge(recip_done, 2 * t + m + 1)
                    nc.vector.tensor_tensor(o_norm[m][0:PAIRP], av[:, :, :, 0:HD],
                                            rc[m][0:PAIRP].unsqueeze(3).broadcast_to([PAIRP, HP, NH, HD]), ALU.mult).then_inc(on_done, 1)

                def step(n, j, prev, ahead):
                    t = n * NW + j
                    last = isinstance(j, int) and j == NW - 1
                    kind = max(0, j - (NW - 3)) if isinstance(j, int) else 0
                    for i in range(NCH):
                        add_bias(t, i, kind)
                        row_max(t, i)
                    dve.wait_ge(v_done, t + 1)
                    src = bank3[PAD:PAIRP, :, 0:HP * C].rearrange("k b (p c) -> k b p c", c=C)
                    odd = v01[:, :, :].rearrange("k (b p a) c -> k a b p c", b=2, a=2)
                    nc.vector.tensor_copy(odd[0:TOK, 1, :, :, 0:HD], src[:, :, :, 0:HD]).then_inc(v_evac_dve, 1)
                    nc.vector.tensor_copy(odd[PAD:PAIRP, 1, :, :, HV:HV + HD], src[:, :, :, HD:2 * HD]).then_inc(v_evac_dve, 1)
                    src2 = bank3[PAD:PAIRP, :, 0:HP * C].rearrange("k b (g o c) -> k o b g c", o=2, c=C)
                    dst2 = v2[:, :, :, :, :].rearrange("k (b g) a o c -> k a o b g c", b=2)
                    nc.vector.tensor_copy(dst2[0:TOK, 1, 0, :, :, 0:HD], src2[:, 0, :, :, 2 * HD:C]).then_inc(v_evac_dve, 1)
                    nc.vector.tensor_copy(dst2[PAD:PAIRP, 1, 1, :, :, 0:HD], src2[:, 1, :, :, 2 * HD:C]).then_inc(v_evac_dve, 1)
                    if prev:
                        residual(t - 1, *before(n, j))
                    if ahead:
                        x_statistics(t + NW, j)
                    if prev:
                        y_statistics(t - 1, j)
                    if last:
                        aggregate(n + 1, (n + 2) * NW, t, ahead)
                    normalise_out(t, 0, 7)
                    if ahead or not last:
                        move_keys(t + 1)
                    normalise_out(t, 1, 3)

                def before(n, j):
                    if isinstance(j, int) and j == 0:
                        return (n - 1, NW - 2), (n - 1, NW - 1)
                    return (n, j - 2), (n, j - 1)

                move_keys(0)
                walk(dve, step, apart=2)
                residual(NI * NW - 1, *before(NI, 0))
                y_statistics(NI * NW - 1, 0)
                aggregate(NI + 1, None, NI * NW, False)

            @block.tensor
            def _(pe):
                pe.wait_ge(psum_ready, 8)
                pe.wait_ge(consts_in, 16 * 11)
                nc.tensor.matmul(bk(7)[C:C + 1, 0:C], b_qkv[:, 2:3], w_proj[0:C, :], start=True, stop=True).then_inc(setup_mm, 1)

                def transposes(strip, done):
                    for w in range(WS):
                        b, at = (3, w) if w < 4 else (4, w - 4)
                        mm = nc.tensor.transpose(bk(b)[0:C, H * at:H * at + H], strip[:, w, :], ident[0:H, 0:H])
                        if w in (3, WS - 1):
                            mm.then_inc(done, 1)

                def transpose_x(n, j):
                    pe.wait_ge(xin_loaded, xin_count(n, j))
                    transposes(xin, xT_done)

                def queries_keys(t):
                    pe.wait_ge(xn_done, t + 1)
                    for b, c0, first in ((5, 0, 0), (6, 0, NP), (3, C, 0), (4, C, NP)):
                        nc.tensor.matmul(bk(b)[0:C, 0:HS], w_qkv[:, c0:c0 + C], xn[:, first:first + NP, 0:TOK],
                                         start=True, stop=True).then_inc(qk_done, 1)

                def scores(i):
                    p0, p1 = CHUNKS[i]
                    for w in range(2 * p0, 2 * p1):
                        a, at = w % 2, NH * TOK * (w // 2 - p0)
                        mm = nc.tensor.matmul(ps_scores[PAD * a:PAD * a + TOK, i, at:at + NH * TOK],
                                              q_sb[:, TOK * w:TOK * w + TOK],
                                              k_sb[:, w, :, :].rearrange("c h k -> c (h k)"), start=True, stop=True)
                    mm.then_inc(scores_done, 1)

                def values():
                    for p in range(NP):
                        mm = nc.tensor.matmul(bank3[0:PAIRP, p // HP, C * (p % HP):C * (p % HP) + C],
                                              xn[:, 2 * p:2 * p + 2, :].rearrange("c a k -> c (a k)")[:, 0:PAIRP],
                                              w_qkv[:, 2 * C:3 * C], start=True, stop=True)
                    mm.then_inc(v_done, 1)

                def transpose_p(m):
                    for p in range(HP):
                        mm = nc.tensor.transpose(bk(5)[0:PAIRP, 128 * p:128 * p + PAIRP],
                                                 p01[0:PAIRP, HP * m + p, :, :].rearrange("q a k -> q (a k)")[:, 0:PAIRP], ident[0:PAIRP, 0:PAIRP])
                    mm.then_inc(pt_done, 1)

                def transpose_p2(m):
                    for g in range(HP // 2):
                        mm = nc.tensor.transpose(bk(6)[0:PAIRP, 128 * g:128 * g + PAIRP],
                                                 p2[0:PAIRP, HP * m + 2 * g:HP * m + 2 * g + 2, :].rearrange("q a k -> q (a k)")[:, 0:PAIRP], ident[0:PAIRP, 0:PAIRP])
                    mm.then_inc(pt_done, 1)

                def weighted_values(m, b):
                    av = bk(b)[:, 0:HP * NH * HV].rearrange("q (p d) -> q p d", p=HP)
                    for p in range(HP):
                        for a in range(2):
                            w = 2 * (HP * m + p) + a
                            rows = slice(PAD * a, PAD * a + TOK)
                            mm = nc.tensor.matmul(av[rows, p, 0:2 * HV], pt01[0:PAIRP, p, a, :], v01[0:PAIRP, w, :], start=True, stop=True)
                            if p % 2:
                                mm = nc.tensor.matmul(av[rows, p - 1:p + 1, 2 * HV:3 * HV], pt2[0:PAIRP, p // 2, a, :],
                                                      v2[0:PAIRP, (HP * m + p) // 2, a, :, :].rearrange("k o c -> k (o c)"), start=True, stop=True)
                    mm.then_inc(av_done, 1)

                def transpose_o(m, b):
                    for p in range(HP):
                        mm = nc.tensor.transpose(bk(b)[0:C, 128 * p:128 * p + PAIRP],
                                                 o_norm[m][0:PAIRP, p, :, :].rearrange("q h d -> q (h d)"), ident[0:PAIRP, 0:PAIRP])
                    mm.then_inc(ot_done, 1)

                def project():
                    for w in range(WS):
                        b, at = (6, w) if w < 4 else (7, w - 4)
                        mm = nc.tensor.matmul(bk(b)[0:H, C * at:C * at + C], oT[:, w, :, :].rearrange("c i h -> c (i h)"), w_proj[:, :], start=True, stop=True)
                        if w in (3, WS - 1):
                            mm.then_inc(proj_done, 1)

                def group_means(i):
                    pe.wait_ge(agg_dve, 3 * i + 1)
                    nc.tensor.matmul(ps_scores[0:C, 0, 500:502], group_sb[:, :], mv[:, :, 0], start=True, stop=True).then_inc(agg_pe, 1)

                def group_spreads(i):
                    pe.wait_ge(agg_dve, 3 * i + 2)
                    nc.tensor.matmul(ps_scores[0:C, 0, 504:506], group_sb[:, :], spread[:, :], start=True, stop=True).then_inc(agg_pe, 1)

                def row_forms(i):
                    pe.wait_ge(agg_copy, 7 * i + 7)
                    for s in range(3):
                        mm = nc.tensor.matmul(bk(4)[:, C * s:C * s + C], stat_bc[:, s, :], ident[0:C, 0:C], start=True, stop=True)
                    mm.then_inc(rows_mm, 1)

                transpose_x(0, 0)
                with pe.Fori(1, NW - 1) as j:
                    pe.wait_ge(xT_evac, 2 * j)
                    pe.wait_ge(x_stats, 2 * j)
                    transpose_x(0, j)
                pe.wait_ge(xT_evac, 2 * (NW - 1))
                pe.wait_ge(x_stats, 2 * (NW - 1))
                transpose_x(0, NW - 1)
                pe.wait_ge(xT_evac, 2 * NW)
                pe.wait_ge(x_stats, 2 * NW)
                group_means(0)
                group_spreads(0)
                pe.wait_ge(consts_ready, 2)
                pe.wait_ge(setup_pool, 15)
                queries_keys(0)

                def step(n, j, prev, ahead):
                    t = n * NW + j
                    last = isinstance(j, int) and j == NW - 1
                    s = t + NW
                    pe.wait_ge(q_evac, 2 * (t + 1))
                    pe.wait_ge(k_evac_act, 2 * len(ACT_KEYS) * (t + 1))
                    pe.wait_ge(k_evac_dve, 2 * len(DVE_KEYS) * (t + 1))
                    if prev:
                        pe.wait_ge(bias_added, NCH * t)
                    for i in range(NCH):
                        scores(i)
                    if prev:
                        pe.wait_ge(on_done, 2 * t)
                        pe.wait_ge(pt_evac, 4 * t)
                        transpose_o(1, 5)
                    if isinstance(j, int) and j == 0 and not (isinstance(n, int) and n == 0):
                        pe.wait_ge(rows_evac, n)
                    values()
                    if prev:
                        pe.wait_ge(ot_evac, 2 * t)
                        project()
                    pe.wait_ge(v_evac_act, 4 * (t + 1))
                    pe.wait_ge(v_evac_dve, 4 * (t + 1))
                    if ahead:
                        transpose_x(n + 1, j)
                    if prev:
                        pe.wait_ge(y_done, 2 * t)
                    pe.wait_ge(exp_done, 2 * NCH * t + 4)
                    transpose_p(0)
                    transpose_p2(0)
                    if ahead:
                        pe.wait_ge(xT_evac, 2 * (s + 1))
                        pe.wait_ge(x_stats, 2 * (s + 1))
                    if prev:
                        transposes(y_strip, yT_done)
                    if last:
                        group_means(n + 1)
                    pe.wait_ge(pt_evac, 4 * t + 2)
                    weighted_values(0, 7)
                    if last:
                        group_spreads(n + 1)
                    if prev:
                        pe.wait_ge(y_stats, 2 * t)
                    more = ahead or not last
                    if more:
                        queries_keys(t + 1)
                        pe.wait_ge(q_evac, 2 * (t + 2))
                    pe.wait_ge(exp_done, 2 * NCH * (t + 1))
                    transpose_p(1)
                    transpose_p2(1)
                    pe.wait_ge(on_done, 2 * t + 1)
                    transpose_o(0, 7)
                    pe.wait_ge(pt_evac, 4 * t + 4)
                    if more:
                        pe.wait_ge(k_evac_act, 2 * len(ACT_KEYS) * (t + 1) + len(ACT_KEYS))
                        pe.wait_ge(k_evac_dve, 2 * len(DVE_KEYS) * (t + 1) + len(DVE_KEYS))
                    weighted_values(1, 3)
                    if last:
                        if more:
                            pe.wait_ge(k_evac_act, 2 * len(ACT_KEYS) * (t + 2))
                            pe.wait_ge(k_evac_dve, 2 * len(DVE_KEYS) * (t + 2))
                        row_forms(n + 1)

                walk(pe, step)
                t = NI * NW
                pe.wait_ge(on_done, 2 * t)
                pe.wait_ge(pt_evac, 4 * t)
                transpose_o(1, 5)
                pe.wait_ge(ot_evac, 2 * t)
                project()
                pe.wait_ge(y_done, 2 * t)
                pe.wait_ge(rows_evac, NI)
                transposes(y_strip, yT_done)
                group_means(NI + 1)
                group_spreads(NI + 1)
                pe.wait_ge(y_stats, 2 * t)
                row_forms(NI + 1)

        phase_c = ExitStack()
        with phase_c:
            band = phase_c.enter_context(nc.sbuf_tensor("band", [128, 2, C, 128], F32))
            y_img = [phase_c.enter_context(nc.sbuf_tensor(f"y_img{u}", [128, BLK * C], F32)) for u in range(2)]
            rows = [phase_c.enter_context(nc.sbuf_tensor(f"rows{u}", [128, 3, C], F32)) for u in range(2)]
            z = [phase_c.enter_context(nc.sbuf_tensor(f"z{u}", [128, CG, BLK], F32)) for u in range(2)]
            v = [phase_c.enter_context(nc.sbuf_tensor(f"v{u}", [128, CG, OUTB], F32)) for u in range(2)]

            POOL_ADDS = [g for g in range(NCG) if g % 3]
            DVE_ADDS = [g for g in range(NCG) if g % 3 == 0]
            HALVES = ((slice(64, 128), 0), (slice(0, 64), NWB))
            MC = 64
            BANKS = 4

            def conv_bank(g):
                return (bk(3), bk(4), bk(5), bk(6))[g % BANKS]

            block = phase_c.enter_context(nc.Block())

            @block.sync
            def _(sp):
                for i in range(4):
                    if i >= 2:
                        sp.wait_ge(band_copied[i % 2], i // 2)
                    sp.dma_start(y_img[i % 2][:, 0:MC * C],
                                 band_dram[i // 2, :, MC * (i % 2):MC * (i % 2) + MC, :].rearrange("p m c -> p (m c)")
                                 ).then_inc(band_in[i % 2], 16)

                def load(n, u):
                    sp.dma_start(rows[u][:, :, :].rearrange("p s c -> p (s c)"),
                                 rows_dram[bass.ds(n + 1, 1), :, :].rearrange("a p c -> (a p) c")).then_inc(y_in[u], 16)
                    img = y_img[u][:, :].rearrange("p (b w c) -> p b w c", w=NWB, c=C)
                    for r in range(PR):
                        for wb in range(NWB):
                            sp.dma_start(img[PC * r:PC * r + PC, :, wb, :],
                                         y_pad[bass.ds(n + 1, 1), r::PR, OC * wb:OC * wb + PC, :].rearrange("a b w c -> w (a b) c")
                                         ).then_inc(y_in[u], 16)

                def store(n, u):
                    img = y_img[u][:, :].rearrange("p (b w c) -> p b w c", w=NWB, c=C)
                    for r in range(PR):
                        row = (r + PR - HALO) % PR
                        b0 = 0 if r >= HALO else 1
                        for wb in range(NWB):
                            sp.dma_start(out[bass.ds(n, 1), row::PR, OC * wb:OC * wb + OC, :].rearrange("a b w c -> w (a b) c"),
                                         img[PC * r + HALO:PC * r + HALO + OC, b0:b0 + NB, wb, :]).then_inc(out_stored, 16)

                for u in range(2):
                    sp.wait_ge(band_copied[u], 2)
                    load(u, u)

                def finish(n, u):
                    sp.wait_ge(added_dve, len(DVE_ADDS) * 2 * (n + 1))
                    sp.wait_ge(added_pool, 2 + len(POOL_ADDS) * 2 * (n + 1))
                    store(n, u)

                with sp.Fori(0, NI // 2 - 1) as k:
                    for u in range(2):
                        n = 2 * k + u
                        finish(n, u)
                        sp.wait_ge(out_stored, 16 * PR * NWB * (n + 1))
                        load(n + 2, u)
                for u in range(2):
                    finish(NI - 2 + u, u)
                sp.wait_ge(out_stored, 16 * PR * NWB * NI)

            @block.scalar
            def _(act):
                for i in (0, 2):
                    act.wait_ge(band_in[0], 16 * (i // 2 + 1))
                    nc.scalar.activation(band[:, i // 2, :, 0:MC], y_img[0][:, 0:MC * C].rearrange("p (m c) -> p c m", c=C),
                                         ACT.Copy, scale=alpha_col).then_inc(band_copied[0], 1)

                def step(n, u):
                    act.wait_ge(y_in[u], 16 * (1 + PR * NWB) * (k_of(n, u) + 1))
                    img = y_img[u][:, :].rearrange("p (b c) -> p c b", c=C)
                    for g in range(NCG):
                        act.wait_ge(gated, 2 * BANKS + 2 * (NCG * n + g - 1))
                        for i in range(CG):
                            c = CG * g + i
                            zz = nc.scalar.activation(z[g % 2][:, i, :], img[:, c, :], ACT.Identity,
                                                      bias=rows[u][:, 2, c:c + 1], scale=rows[u][:, 1, c:c + 1])
                        zz.then_inc(z_ready, 1)

                with act.Fori(0, NI // 2) as k:
                    def k_of(n, u):
                        return k
                    for u in range(2):
                        step(2 * k + u, u)

            @block.tensor
            def _(pe):
                pe.wait_ge(band_copied[0], 2)
                pe.wait_ge(band_copied[1], 2)
                with pe.Fori(0, NI // 2) as k:
                    for u in range(2):
                        n = 2 * k + u
                        for g in range(NCG):
                            pe.wait_ge(z_ready, NCG * n + g + 1)
                            pe.wait_ge(gated, 2 * (NCG * n + g) + 2)
                            for i in range(CG):
                                o = conv_bank(g)[:, OUTB * i:OUTB * i + OUTB]
                                nc.tensor.matmul(o, band[:, 0, CG * g + i, :], z[g % 2][:, i, 0:OUTB], start=True, stop=False)
                                mm = nc.tensor.matmul(o, band[:, 1, CG * g + i, :], z[g % 2][:, i, NWB:NWB + OUTB], start=False, stop=True)
                            mm.then_inc(conv_done, 1)

            def add_group(engine, u, g, done):
                img = y_img[u][:, :].rearrange("p (b c) -> p c b", c=C)
                for rows_, b0 in HALVES:
                    part = img[rows_, CG * g:CG * g + CG, b0:b0 + OUTB]
                    engine.tensor_tensor(part, v[g % 2][rows_, :, :], part, ALU.add).then_inc(done, 1)

            @block.vector
            def _(dve):
                for i in (1, 3):
                    dve.wait_ge(band_in[1], 16 * (i // 2 + 1))
                    nc.vector.tensor_scalar(band[:, i // 2, :, MC:2 * MC], y_img[1][:, 0:MC * C].rearrange("p (m c) -> p c m", c=C),
                                            alpha_col, None, ALU.mult).then_inc(band_copied[1], 1)
                for g in range(BANKS):
                    nc.vector.memset(conv_bank(g)[:, :], 0.0).then_inc(gated, 2)
                with dve.Fori(0, NI // 2) as k:
                    for u in range(2):
                        n = 2 * k + u
                        for g in range(NCG):
                            dve.wait_ge(conv_done, NCG * n + g + 1)
                            dve.wait_ge(added_pool, 2 + 2 * (len(POOL_ADDS) * n + len([q for q in POOL_ADDS if q <= g - 2])))
                            if g - 2 in DVE_ADDS:
                                dve.wait_ge(added_dve, 2 * (len(DVE_ADDS) * n + len([q for q in DVE_ADDS if q <= g - 2])))
                            for rows_, b0 in HALVES:
                                nc.vector.scalar_tensor_tensor(
                                    v[g % 2][rows_, :, :], conv_bank(g)[rows_, 0:CG * OUTB].rearrange("p (c b) -> p c b", c=CG),
                                    gate_one[rows_, :], z[g % 2][rows_, :, b0:b0 + OUTB], ALU.add, ALU.mult).then_inc(gated, 1)
                            if g in DVE_ADDS:
                                dve.wait_ge(gated, 2 * BANKS + 2 * (NCG * n + g + 1))
                                add_group(nc.vector, u, g, added_dve)

            @block.gpsimd
            def _(pool):
                for q in range(2):
                    nc.gpsimd.memset(v[q][:, :, :], 0.0).then_inc(added_pool, 1)
                with pool.Fori(0, NI // 2) as k:
                    for u in range(2):
                        n = 2 * k + u
                        for g in POOL_ADDS:
                            pool.wait_ge(gated, 2 * BANKS + 2 * (NCG * n + g + 1))
                            add_group(nc.gpsimd, u, g, added_pool)


def host_bias_windows(table):
    import numpy as np
    flipped = table.reshape(2 * WS - 1, 2 * WS - 1, NH)[::-1, ::-1]
    last = WS - 1
    win = [flipped[last - h:last - h + WS, last - w:last - w + WS].transpose(2, 1, 0).reshape(NH, TOK)
           for w in range(WS) for h in range(WS)]
    return np.stack(win)


def host_masks():
    import numpy as np
    side = np.repeat([0, 1, 2], [H - WS, WS - SS, SS])
    side = np.roll(side, -SS).reshape(NW, WS)
    m = np.zeros((PAIRP, 3, 2, TOK), np.float32)
    for k, column in enumerate((0, NW - 2, NW - 1)):
        for i, (upper, lower) in enumerate(((0, 1), (NW - 2, NW - 1))):
            for start, row in ((0, upper), (PAD, lower)):
                region = (side[column][:, None] + 3 * side[row][None, :]).reshape(TOK)
                m[start:start + TOK, k, i] = np.where(region[:, None] != region[None, :], np.float32(-1e9), np.float32(0))
    return m


def kernel(x, L0_conv_qkv_w, L0_conv_qkv_b, L0_conv_proj_w, L0_conv_proj_b, L0_conv_bias_table,
           L1_conv_kernel, L1_conv_alpha, L1_conv_bias):
    import numpy as np
    import concourse.bacc as bacc
    from concourse.bass_utils import run_bass_kernel_spmd

    nc = bacc.Bacc("TRN2", target_bir_lowering=False, num_devices=1)
    arrays = {
        "x": x,
        "qkv_w": L0_conv_qkv_w,
        "qkv_b": np.asarray(L0_conv_qkv_b).reshape(3, C).T,
        "proj_w": L0_conv_proj_w,
        "proj_b": np.asarray(L0_conv_proj_b).reshape(1, C),
        "bias_win": host_bias_windows(np.asarray(L0_conv_bias_table)),
        "taps": L1_conv_kernel,
        "alpha": L1_conv_alpha,
        "bias": L1_conv_bias,
        "masks": host_masks(),
        "eye": np.eye(128, dtype=np.float32),
        "group": np.kron(np.eye(C // 3, dtype=np.float32), np.full((3, 3), 1 / 3, np.float32)),
    }
    arrays = {f"in_{k}": np.ascontiguousarray(a) for k, a in arrays.items()}
    aps = [nc.dram_tensor(k, a.shape, F32, kind="ExternalInput").ap() for k, a in arrays.items()]
    out = nc.dram_tensor("out", (NI, H, W, C), F32, kind="ExternalOutput").ap()
    attention_then_conv(nc, *aps, out)
    return run_bass_kernel_spmd(nc, [arrays], core_ids=[0]).results[0]["out"]
```

```python
from contextlib import ExitStack

import concourse.bass as bass
from concourse import mybir

F32 = mybir.dt.float32
ALU = mybir.AluOpType
ACT = mybir.ActivationFunctionType
AX_X = mybir.AxisListType.X

NI, H, W, C = 32, 112, 112, 96
WS, SS, NH = 7, 3, 3
HD = C // NH
NW = H // WS
TOK = WS * WS
PAD = 64
PAIRP = PAD + TOK
STRIP = NW * TOK
NP = NW // 2
PB = 512 // (NH * TOK)
CHUNKS = [(p, min(p + PB, NP)) for p in range(0, NP, PB)]
NCH = len(CHUNKS)
HP = NP // 2
HS = STRIP // 2
HV = HD + 1
SCALE = float(HD) ** -0.5
EPS = 1e-5
KS = 5
HALO = KS // 2
N_BAND = KS * KS * 4
PR, PC = 4, 32
OC = PC - KS + 1
NB, NWB = H // PR, W // OC
HB, WP = H + KS - 1, W + KS - 1
BLK = (NB + 1) * NWB
OUTB = NB * NWB
CG = 4
NCG = C // CG
ROWS = 3 * C
ROW_CUTS = [(0, SS, 96), (96, SS + 96, H - SS - 96), (H - SS, 0, SS)]


def attention_then_conv(nc, x, qkv_w, qkv_b, proj_w, proj_b, bias_win, taps, alpha, bias, masks, eye, group, out):
    y_pad = nc.dram_tensor("y_pad", (NI + 1, HB, WP, C), F32, kind="Internal").ap()
    rows_dram = nc.dram_tensor("rows_dram", (NI + 1, 128, ROWS), F32, kind="Internal").ap()
    band_dram = nc.dram_tensor("band_dram", (2, 128, 128, C), F32, kind="Internal").ap()

    ctx = ExitStack()
    with ctx:
        def sb(name, shape, space=ctx):
            return space.enter_context(nc.sbuf_tensor(name, shape, F32))

        def sem(name):
            return ctx.enter_context(nc.semaphore(name))

        ps_scores = ctx.enter_context(nc.psum_tensor("ps_scores", [128, NCH, 512], F32))
        bank3 = ctx.enter_context(nc.psum_tensor("bank34", [128, 2, 512], F32))
        bank = {b: ctx.enter_context(nc.psum_tensor(f"bank{b}", [128, 512], F32)) for b in (5, 6, 7)}

        def q_bank(i):
            return ps_scores[:, 1 + i, :]

        def bk(b):
            return bank3[:, b - 3, :] if b < 5 else bank[b][:, :]

        ident = sb("ident", [128, 128])
        small = sb("small", [128, 16])
        alpha_col, gate_one = small[:, 0:1], small[:, 1:2]

        consts_in, consts_ready, zeros_ready, psum_ready = sem("consts_in"), sem("consts_ready"), sem("zeros_ready"), sem("psum_ready")
        setup_mm, setup_dve, setup_pool = sem("setup_mm"), sem("setup_dve"), sem("setup_pool")
        band_zeroed, band_written = sem("band_zeroed"), sem("band_written")
        xin_loaded, xres_loaded, y_stored = sem("xin_loaded"), sem("xres_loaded"), sem("y_stored")
        xT_done, xT_evac, x_stats = sem("xT_done"), sem("xT_evac"), sem("x_stats")
        xn_done, qk_done, q_evac_act, q_evac_dve, k_evac_act, k_evac_dve = (
            sem("xn_done"), sem("qk_done"), sem("q_evac_act"), sem("q_evac_dve"), sem("k_evac_act"), sem("k_evac_dve"))
        v_done, v_evac_act, v_evac_dve = sem("v_done"), sem("v_evac_act"), sem("v_evac_dve")
        scores_done, bias_added, max_done, sub_done, exp_done = (
            sem("scores_done"), sem("bias_added"), sem("max_done"), sem("sub_done"), sem("exp_done"))
        pt_done, pt_evac, av_done, recip_done, on_done = (
            sem("pt_done"), sem("pt_evac"), sem("av_done"), sem("recip_done"), sem("on_done"))
        ot_done, ot_evac, proj_done, y_done, yT_done, y_stats = (
            sem("ot_done"), sem("ot_evac"), sem("proj_done"), sem("y_done"), sem("yT_done"), sem("y_stats"))
        agg_dve, agg_pe, agg_pool, norm_ready, bc_ready = (
            sem("agg_dve"), sem("agg_pe"), sem("agg_pool"), sem("norm_ready"), sem("bc_ready"))
        agg_copy = sem("agg_copy")
        rows_mm, rows_evac, rows_stored = sem("rows_mm"), sem("rows_evac"), sem("rows_stored")
        band_in, band_copied = [sem("band_in0"), sem("band_in1")], [sem("band_copied0"), sem("band_copied1")]
        y_in = [sem("y_in0"), sem("y_in1")]
        z_ready, conv_done, gated, added_dve, added_pool, out_stored = (
            sem("z_ready"), sem("conv_done"), sem("gated"), sem("added_dve"), sem("added_pool"), sem("out_stored"))

        phase_b = ExitStack()
        with phase_b:
            def sbb(name, shape):
                return sb(name, shape, phase_b)

            xT = sbb("xT", [C, NW, NW, WS, WS])
            xin = sbb("xin", [H, WS, C])
            xres = sbb("xres", [H, WS, C])
            y_strip = sbb("y_strip", [H, WS, C])
            xn = sbb("xn", [C, NW, PAD])
            q_sb = sbb("q_sb", [C, STRIP])
            k_sb = sbb("k_sb", [C, NW, NH, TOK])
            v01 = sbb("v01", [128, NW, 2 * HV])
            v2 = sbb("v2", [128, HP, 2, 2, HV])
            t_sb = sbb("t_sb", [128, NP, NH, TOK])
            mx = sbb("mx", [128, NP, NH])
            p01 = sbb("p01", [128, NP, 2, PAD])
            p2 = sbb("p2", [128, NP, PAD])
            pt01 = sbb("pt01", [128, HP, 2, TOK])
            pt2 = sbb("pt2", [128, HP // 2, 2, TOK])
            rc = [sbb(f"rc{m}", [128, HP, NH]) for m in range(2)]
            o_norm = [sbb(f"o_norm{m}", [128, HP, NH, HD]) for m in range(2)]
            oT = sbb("oT", [C + 1, WS, NW, WS])
            bias_sb = sbb("bias_sb", [128, 3, NP, NH, TOK])
            bias_base = sbb("bias_base", [128, NH, TOK])
            mask_sb = sbb("mask_sb", [128, 3, 2, TOK])
            w_qkv = sbb("w_qkv", [C, 3 * C])
            w_proj = sbb("w_proj", [C + 1, C])
            b_qkv = sbb("b_qkv", [C, 3])
            b_proj = sbb("b_proj", [C + 1, C])
            group_sb = sbb("group_sb", [C, C])
            x_bn = sbb("x_bn", [C, NW, 2, 6])
            y_bn = sbb("y_bn", [C, NW, 2, 6])
            y_agg_in = sbb("y_agg_in", [C, NW, 2, 6])
            mv = sbb("mv", [C, 2, 2])
            dev = sbb("dev", [C, 2])
            spread = sbb("spread", [C, 2])
            var_eps = sbb("var_eps", [C, 2])
            carrier = sbb("carrier", [C, 1])
            minus_half = sbb("minus_half", [C, 2])
            stat = sbb("stat", [C, 3, 2])
            stat_bc = sbb("stat_bc", [C, 3, 128])
            rows_sb = sbb("rows_sb", [128, ROWS])
            zeros = sbb("zeros", [128, 16 * C])

            b_q_scaled = small[0:C, 2:3]
            def xin_count(n, j):
                return 16 * len(ROW_CUTS) * ((NW + 1) * n + j + 1) + (16 * len(ROW_CUTS) if isinstance(j, int) and j == NW - 1 else 0)

            ACT_KEYS, DVE_KEYS = (0, 1), (2,)

            def key_block(i, b, h):
                rows_ = slice(HD * h, HD * h + HD)
                return (rows_, bk(b)[rows_, 0:HS].rearrange("c (w k) -> c w k", k=TOK),
                        k_sb[rows_, NP * i:NP * i + NP, h, :])

            block = phase_b.enter_context(nc.Block())

            def walk(eng, step):
                def image(n, prev, ahead, last_ahead):
                    step(n, 0, prev, ahead)
                    if not prev:
                        step(n, 1, True, ahead)
                    with eng.Fori(1 if prev else 2, NW - 2) as j:
                        step(n, j, True, ahead)
                    step(n, NW - 2, True, ahead)
                    step(n, NW - 1, True, last_ahead)

                image(0, False, True, True)
                with eng.Fori(1, NI - 2) as n:
                    image(n, True, True, True)
                image(NI - 2, True, True, False)
                image(NI - 1, True, False, False)

            def ahead_of(n, j):
                if isinstance(j, int) and j == NW - 1:
                    return n + 2, 0
                return n + 1, j + 1

            @block.sync
            def _(sp):
                sp.dma_start(ident[:, :], eye).then_inc(consts_in, 16)
                sp.dma_start(w_qkv[:, :], qkv_w).then_inc(consts_in, 16)
                sp.dma_start(w_proj[0:C, :], proj_w).then_inc(consts_in, 16)
                sp.dma_start(b_qkv[:, :], qkv_b).then_inc(consts_in, 16)
                sp.dma_start(b_proj[C:C + 1, :], proj_b).then_inc(consts_in, 16)
                for lo in (0, PAD):
                    if lo == 0:
                        sp.wait_ge(zeros_ready, 1)
                    sp.dma_start(bias_base[lo:lo + TOK, :, :], bias_win).then_inc(consts_in, 16)
                sp.dma_start(mask_sb[0:PAIRP, :, :, :], masks).then_inc(consts_in, 16)
                sp.dma_start(group_sb[:, :], group).then_inc(consts_in, 16)
                sp.dma_start(alpha_col, alpha.broadcast_to([128, 1])).then_inc(consts_in, 16)
                sp.dma_start(gate_one, bias.broadcast_to([128, 1])).then_inc(consts_in, 16)

                def column_cuts(j):
                    if isinstance(j, int) and j == NW - 1:
                        return [(0, WS * j + SS, W - WS * j - SS), (W - WS * j - SS, 0, SS)]
                    return [(0, WS * j + SS, WS)]

                def load(dst, n, j, done):
                    for p0, r0, nr in ROW_CUTS:
                        for w0, c0, ncol in column_cuts(j):
                            sp.dma_start(dst[p0:p0 + nr, w0:w0 + ncol, :],
                                         x[bass.ds(n, 1), r0:r0 + nr, bass.ds(c0, ncol), :].rearrange("a r w c -> (a r) w c")
                                         ).then_inc(done, 16)

                def store(n, j):
                    for p0, r0, nr in ROW_CUTS:
                        for w0, c0, ncol in column_cuts(j):
                            sp.dma_start(y_pad[bass.ds(n + 1, 1), r0 + HALO:r0 + HALO + nr, bass.ds(c0 + HALO, ncol), :]
                                         .rearrange("a r w c -> (a r) w c"),
                                         y_strip[p0:p0 + nr, w0:w0 + ncol, :]).then_inc(y_stored, 16)

                def stage(n, j, prev, ahead):
                    t = n * NW + j
                    if ahead:
                        sp.wait_ge(xT_done, 2 * (t + NW + 1))
                        load(xin, *ahead_of(n, j), xin_loaded)
                    if prev:
                        sp.wait_ge(y_done, 2 * t)
                        if isinstance(j, int) and j == 0:
                            store(n - 1, NW - 1)
                        else:
                            store(n, j - 1)
                    load(xres, n, j, xres_loaded)
                    if isinstance(j, int) and j == NW - 1:
                        save_rows(n)

                def save_rows(n):
                    sp.wait_ge(rows_evac, n + 1)
                    sp.dma_start(rows_dram[bass.ds(n, 1), :, :].rearrange("a p c -> (a p) c"), rows_sb[:, :]).then_inc(rows_stored, 16)
                    image = y_pad[bass.ds(n, 1), :, :, :]
                    for e in (0, 1, HB - 2, HB - 1):
                        sp.dma_start(image[:, e, :, :].rearrange("a w c -> (a w) c"), rows_sb[0:WP, 0:C]).then_inc(rows_stored, 16)
                        sp.dma_start(image[:, 2:HB - 2, e, :].rearrange("a r c -> (a r) c"), rows_sb[0:H, 0:C]).then_inc(rows_stored, 16)

                load(xin, 0, 0, xin_loaded)
                with sp.Fori(1, NW - 1) as j:
                    sp.wait_ge(xT_done, 2 * j)
                    load(xin, 0, j, xin_loaded)
                sp.wait_ge(xT_done, 2 * (NW - 1))
                load(xin, 0, NW - 1, xin_loaded)

                sp.wait_ge(xT_done, 2 * NW)
                load(xin, 1, 0, xin_loaded)

                walk(sp, stage)
                sp.wait_ge(y_done, 2 * NI * NW)
                store(NI - 1, NW - 1)
                save_rows(NI)
                sp.wait_ge(y_stored, xin_count(NI - 1, NW - 1))
                sp.wait_ge(rows_stored, 16 * 9 * (NI + 1))
                sp.wait_ge(band_written, 16 * N_BAND)

            @block.gpsimd
            def _(pool):
                nc.gpsimd.memset(zeros[:, :], 0.0).then_inc(setup_pool, 1)
                nc.gpsimd.memset(bias_base[:, :, :], 0.0).then_inc(zeros_ready, 1)
                nc.gpsimd.memset(xn[:, :, :], 0.0).then_inc(setup_pool, 1)
                nc.gpsimd.memset(v01[:, :, :], 0.0).then_inc(setup_pool, 1)
                nc.gpsimd.memset(k_sb[:, :, :, :], 0.0).then_inc(setup_pool, 1)
                nc.gpsimd.memset(v2[:, :, :, :, :], 0.0).then_inc(setup_pool, 1)
                nc.gpsimd.memset(p01[:, :, :, :], 0.0).then_inc(setup_pool, 1)
                nc.gpsimd.memset(p2[:, :, :], 0.0).then_inc(setup_pool, 1)
                nc.gpsimd.memset(y_bn[:, :, :, :], 1.0).then_inc(setup_pool, 1)
                nc.gpsimd.memset(y_agg_in[:, :, :, :], 1.0).then_inc(setup_pool, 1)
                nc.gpsimd.memset(minus_half[:, :], -0.5).then_inc(setup_pool, 1)
                pool.wait_ge(setup_pool, 10)
                nc.gpsimd.memset(oT[C:C + 1, :, :, :], 1.0).then_inc(setup_pool, 1)
                for i, lo in enumerate((0, PAD)):
                    pool.wait_ge(setup_pool, 11 + 2 * i)
                    nc.gpsimd.memset(v01[lo:lo + PAD, :, HV * i + HD:HV * i + HV], 1.0).then_inc(setup_pool, 1)
                    pool.wait_ge(setup_pool, 12 + 2 * i)
                    nc.gpsimd.memset(v2[lo:lo + PAD, :, :, i, HD:HV], 1.0).then_inc(setup_pool, 1)
                for half in range(2):
                    for g in range(128 // 16):
                        pool.dma_start(band_dram[half, :, 16 * g:16 * g + 16, :].rearrange("p m c -> p (m c)"),
                                       zeros[:, :]).then_inc(band_zeroed, 16)
                pool.wait_ge(band_zeroed, 16 * 16)
                for dy in range(KS):
                    for dx in range(KS):
                        for r in range(PR):
                            half, row = (r + dy) // PR, (r + dy) % PR
                            col = (r + KS // 2) % PR * PC + KS // 2
                            start = band_dram[half, row * PC + dx, col, 0:1]
                            diagonal = bass.AP(band_dram.tensor, start.offset, [[(128 + 1) * C, OC], [1, C]])
                            tap = taps[dy, dx:dx + 1, :].broadcast_to([OC, C])
                            pool.dma_start(diagonal, tap).then_inc(band_written, 16)

                def subtract(t, i):
                    p0, p1 = CHUNKS[i]
                    pool.wait_ge(max_done, NCH * t + i + 1)
                    nc.gpsimd.tensor_tensor(t_sb[0:PAIRP, p0:p1], t_sb[0:PAIRP, p0:p1],
                                            mx[0:PAIRP, p0:p1].unsqueeze(3).broadcast_to([PAIRP, p1 - p0, NH, TOK]),
                                            ALU.subtract).then_inc(sub_done, 1)

                def power(i):
                    pool.wait_ge(agg_dve, 3 * (i + 1))
                    nc.gpsimd.tensor_tensor(stat[:, 1, :], var_eps[:, :], minus_half[:, :], ALU.pow).then_inc(agg_pool, 1)

                power(0)

                def step(n, j, prev, ahead):
                    t = n * NW + j
                    for i in range(NCH):
                        subtract(t, i)
                    if isinstance(j, int) and j == NW - 2:
                        power(n + 1)

                walk(pool, step)
                power(NI + 1)

            @block.scalar
            def _(act):
                act.wait_ge(consts_ready, 2)
                act.wait_ge(setup_pool, 15)

                def evac_xT(s, slot, b, waited=False):
                    w0, w1 = ((0, 4), (4, WS))[b]
                    if not waited:
                        act.wait_ge(xT_done, 2 * s + b + 1)
                    src = bk(3 + b)[0:C, 0:H * (w1 - w0)].rearrange("c (w i h) -> c w i h", i=NW, h=WS)
                    dst = xT[:, bass.ds(slot, 1), :, w0:w1, :].rearrange("c a i w h -> c w (a i) h")
                    nc.scalar.activation(dst, src, ACT.Copy).then_inc(xT_evac, 1)

                def normalise(t, slot, image):
                    act.wait_ge(norm_ready, image + 1)
                    act.wait_ge(xT_evac, 2 * (t + 1))
                    if not (isinstance(t, int) and t == 0):
                        act.wait_ge(v_done, t)
                    src = xT[:, bass.ds(slot, 1), :, :, :].rearrange("c a i w h -> c (a i) (w h)")
                    nc.scalar.activation(xn[:, :, 0:TOK], src, ACT.Identity, bias=stat[:, 2, 0:1],
                                         scale=stat[:, 1, 0:1]).then_inc(xn_done, 1)

                def evac_q(t, i):
                    act.wait_ge(qk_done, 4 * t + i + 1)
                    nc.scalar.activation(q_sb[:, HS * i:HS * i + HS], q_bank(i)[0:C, 0:HS], ACT.Identity,
                                         bias=b_q_scaled, scale=SCALE).then_inc(q_evac_act, 1)

                def evac_k(t, i):
                    act.wait_ge(qk_done, 4 * t + i + 3)
                    for h in ACT_KEYS:
                        rows_, src, dst = key_block(i, 3 + i, h)
                        nc.scalar.activation(dst, src, ACT.Identity, bias=b_qkv[rows_, 1:2]).then_inc(k_evac_act, 1)

                def evac_oT(t, m, b):
                    act.wait_ge(ot_done, 2 * t + m + 1)
                    src = bk(b)[0:C, :].rearrange("c (i k) -> c i k", k=PAD)[:, :, 0:TOK].rearrange("c i (w h) -> c i w h", h=WS)
                    dst = oT[0:C, :, NP * m:NP * m + NP, :].rearrange("c w i h -> c i w h")
                    nc.scalar.activation(dst, src, ACT.Copy).then_inc(ot_evac, 1)

                def exps(t, i):
                    p0, p1 = CHUNKS[i]
                    act.wait_ge(sub_done, NCH * t + i + 1)
                    nc.scalar.activation(p01[0:PAIRP, p0:p1, :, 0:TOK], t_sb[0:PAIRP, p0:p1, 0:2], ACT.Exp).then_inc(exp_done, 1)
                    nc.scalar.activation(p2[0:PAIRP, p0:p1, 0:TOK], t_sb[0:PAIRP, p0:p1, 2], ACT.Exp).then_inc(exp_done, 1)

                def evac_pt(t, m):
                    for i, (b, dst, cnt) in enumerate(((5, pt01, HP), (6, pt2, HP // 2))):
                        act.wait_ge(pt_done, 4 * t + 2 * m + i + 1)
                        src = bk(b)[0:PAIRP, 0:128 * cnt].rearrange("k (p a q) -> k p a q", p=cnt, q=PAD)[:, :, :, 0:TOK]
                        nc.scalar.activation(dst[0:PAIRP, :, :, :], src, ACT.Copy).then_inc(pt_evac, 1)

                with act.Fori(0, NW) as j:
                    evac_xT(j, j, 0)
                    evac_xT(j, j, 1)
                normalise(0, 0, 0)
                act.wait_ge(xn_done, 1)
                for b in range(2):
                    evac_xT(NW, 0, b)
                evac_q(0, 1)
                evac_k(0, 0)
                evac_k(0, 1)

                def step(n, j, prev, ahead):
                    t = n * NW + j
                    last = isinstance(j, int) and j == NW - 1
                    exps(t, 0)
                    if prev:
                        evac_oT(t - 1, 1, 5)
                    act.wait_ge(v_done, t + 1)
                    src = bank3[0:TOK, :, 0:HP * C].rearrange("k b (p c) -> k b p c", c=C)
                    even = v01[:, :, :].rearrange("k (b p a) c -> k a b p c", b=2, a=2)
                    nc.scalar.activation(even[0:TOK, 0, :, :, 0:HD], src[:, :, :, 0:HD], ACT.Copy).then_inc(v_evac_act, 1)
                    nc.scalar.activation(even[PAD:PAIRP, 0, :, :, HV:HV + HD], src[:, :, :, HD:2 * HD], ACT.Copy).then_inc(v_evac_act, 1)
                    src2 = bank3[0:TOK, :, 0:HP * C].rearrange("k b (g o c) -> k o b g c", o=2, c=C)
                    dst2 = v2[:, :, :, :, :].rearrange("k (b g) a o c -> k a o b g c", b=2)
                    nc.scalar.activation(dst2[0:TOK, 0, 0, :, :, 0:HD], src2[:, 0, :, :, 2 * HD:C], ACT.Copy).then_inc(v_evac_act, 1)
                    nc.scalar.activation(dst2[PAD:PAIRP, 0, 1, :, :, 0:HD], src2[:, 1, :, :, 2 * HD:C], ACT.Copy).then_inc(v_evac_act, 1)
                    exps(t, 1)
                    more = not (last and isinstance(n, int) and n == NI - 1)
                    if more:
                        normalise(t + 1, 0 if last else j + 1, n + 1 if last else n)
                    if ahead:
                        act.wait_ge(xn_done, t + 2)
                        act.wait_ge(xT_done, 2 * (t + NW + 1) + 1)
                    evac_pt(t, 0)
                    if ahead:
                        evac_xT(t + NW + 1, ahead_of(n, j)[1], 0, waited=True)
                        evac_xT(t + NW + 1, ahead_of(n, j)[1], 1)
                    exps(t, 2)
                    if last:
                        rows_out(n)
                    if more:
                        evac_q(t + 1, 1)
                        evac_k(t + 1, 0)
                        evac_k(t + 1, 1)
                    evac_pt(t, 1)
                    evac_oT(t, 0, 7)

                def rows_out(n):
                    act.wait_ge(rows_mm, n + 1)
                    if not (isinstance(n, int) and n == 0):
                        act.wait_ge(rows_stored, 16 * 9 * n)
                    nc.scalar.activation(rows_sb[:, :], ps_scores[:, 0, 0:ROWS], ACT.Copy).then_inc(rows_evac, 1)

                walk(act, step)
                evac_oT(NI * NW - 1, 1, 5)
                rows_out(NI)

            @block.vector
            def _(dve):
                for b in range(NCH):
                    nc.vector.memset(ps_scores[:, b, :], 1.0).then_inc(psum_ready, 1)
                for b in (3, 4, 5, 6, 7):
                    nc.vector.memset(bk(b), 1.0).then_inc(psum_ready, 1)
                dve.wait_ge(consts_in, 16 * 11)
                nc.vector.tensor_scalar(b_q_scaled, b_qkv[:, 0:1], SCALE, None, ALU.mult).then_inc(consts_ready, 1)
                nc.vector.tensor_scalar(gate_one, gate_one, 1.0, None, ALU.add).then_inc(setup_dve, 1)
                for k in range(3):
                    for p in range(NP):
                        nc.vector.tensor_tensor(bias_sb[0:PAIRP, k, p, :, :], bias_base[0:PAIRP, :, :],
                                                mask_sb[0:PAIRP, k, int(p == NP - 1), :].unsqueeze(1).broadcast_to([PAIRP, NH, TOK]),
                                                ALU.add).then_inc(setup_dve, 1)
                dve.wait_ge(setup_mm, 1)
                nc.vector.tensor_tensor(w_proj[C:C + 1, :], bk(7)[C:C + 1, 0:C], b_proj[C:C + 1, :], ALU.add).then_inc(consts_ready, 1)
                dve.wait_ge(setup_dve, 1 + 3 * NP)
                dve.wait_ge(setup_pool, 15)

                def x_statistics(s, slot):
                    dve.wait_ge(xT_evac, 2 * s + 2)
                    for b in range(2):
                        nc.vector.bn_stats(x_bn[:, bass.ds(slot, 1), b, :].rearrange("c a s -> c (a s)"),
                                           xT[:, bass.ds(slot, 1), NP * b:NP * b + NP, :, :].rearrange("c a i w h -> c (a i w h)")
                                           ).then_inc(x_stats, 1)

                def y_statistics(t, slot):
                    for b, wn in enumerate((4, WS - 4)):
                        dve.wait_ge(yT_done, 2 * t + b + 1)
                        nc.vector.bn_stats(y_bn[:, bass.ds(slot, 1), b, :].rearrange("c a s -> c (a s)"),
                                           bk(3 + b)[0:C, 0:H * wn]).then_inc(y_stats, 1)

                def channel_statistics(i, s, of_x):
                    nc.vector.tensor_copy(y_agg_in[:, NW - 1, :, :], y_bn[:, 0, :, :]).then_inc(agg_copy, 1)
                    if of_x:
                        dve.wait_ge(x_stats, 2 * s)
                        nc.vector.memset(carrier[:, :], 0.0)
                    nc.vector.bn_aggr(mv[:, 0, :], x_bn[:, :, :, :].rearrange("c a b s -> c (a b s)")).then_inc(agg_copy, 1)
                    dve.wait_ge(agg_copy, 7 * i + 2)
                    nc.vector.memset(carrier[:, :], 0.0)
                    nc.vector.bn_aggr(mv[:, 1, :], y_agg_in[:, :, :, :].rearrange("c a b s -> c (a b s)")).then_inc(agg_dve, 1)

                def channel_spread(i):
                    dve.wait_ge(agg_pe, 2 * i + 1)
                    nc.vector.tensor_copy(stat[:, 0, :], ps_scores[0:C, 0, 500:502]).then_inc(agg_copy, 1)
                    nc.vector.tensor_tensor(dev[:, :], mv[:, :, 0], ps_scores[0:C, 0, 500:502], ALU.subtract).then_inc(agg_copy, 1)
                    dve.wait_ge(agg_copy, 7 * i + 4)
                    nc.vector.tensor_tensor(spread[:, :], dev[:, :], dev[:, :], ALU.mult).then_inc(agg_copy, 1)
                    dve.wait_ge(agg_copy, 7 * i + 5)
                    nc.vector.tensor_tensor(spread[:, :], spread[:, :], mv[:, :, 1], ALU.add).then_inc(agg_dve, 1)

                def group_variance(i):
                    dve.wait_ge(agg_pe, 2 * i + 2)
                    nc.vector.tensor_scalar(var_eps[:, :], ps_scores[0:C, 0, 504:506], EPS, None, ALU.add).then_inc(agg_dve, 1)

                def scale_and_shift(i):
                    dve.wait_ge(agg_pool, i + 1)
                    nc.vector.scalar_tensor_tensor(stat[:, 2, :], stat[:, 0, :], -1.0, stat[:, 1, :], ALU.mult, ALU.mult).then_inc(norm_ready, 1)

                def keep_y_statistics(i, t):
                    if t is not None:
                        dve.wait_ge(y_stats, 2 * t)
                    nc.vector.tensor_copy(y_agg_in[:, 0:NW - 1, :, :], y_bn[:, 1:NW, :, :]).then_inc(agg_copy, 1)

                def broadcast_y_statistics(i):
                    dve.wait_ge(norm_ready, i + 1)
                    nc.vector.tensor_copy(stat_bc[:, :, :], stat[:, :, 1:2].broadcast_to([C, 3, 128])).then_inc(agg_copy, 1)

                def all_statistics(i, s, t, of_x):
                    channel_statistics(i, s, of_x)
                    channel_spread(i)
                    group_variance(i)
                    scale_and_shift(i)
                    broadcast_y_statistics(i)
                    keep_y_statistics(i, t)

                with dve.Fori(0, NW) as j:
                    x_statistics(j, j)
                all_statistics(0, NW, None, True)
                x_statistics(NW, 0)

                def add_bias(t, i, kind):
                    p0, p1 = CHUNKS[i]
                    dve.wait_ge(scores_done, NCH * t + i + 1)
                    nc.vector.tensor_tensor(
                        t_sb[0:PAIRP, p0:p1].rearrange("q p h k -> q (p h k)"), ps_scores[0:PAIRP, i, 0:NH * TOK * (p1 - p0)],
                        bias_sb[0:PAIRP, kind, p0:p1].rearrange("q p h k -> q (p h k)"), ALU.add).then_inc(bias_added, 1)

                def row_max(t, i):
                    p0, p1 = CHUNKS[i]
                    dve.wait_ge(bias_added, NCH * t + i + 1)
                    nc.vector.tensor_reduce(mx[0:PAIRP, p0:p1], t_sb[0:PAIRP, p0:p1], AX_X, ALU.max).then_inc(max_done, 1)

                def move_queries(t):
                    dve.wait_ge(qk_done, 4 * t + 1)
                    nc.vector.tensor_scalar(q_sb[:, 0:HS], q_bank(0)[0:C, 0:HS], SCALE, b_q_scaled, ALU.mult, ALU.add).then_inc(q_evac_dve, 1)

                def move_keys(t):
                    for i, b in enumerate((3, 4)):
                        dve.wait_ge(qk_done, 4 * t + i + 3)
                        for h in DVE_KEYS:
                            rows_, src, dst = key_block(i, b, h)
                            nc.vector.tensor_scalar(dst, src, b_qkv[rows_, 1:2], None, ALU.add).then_inc(k_evac_dve, 1)

                def residual(t, last, this):
                    dve.wait_ge(xres_loaded, xin_count(*this))
                    if not (isinstance(t, int) and t == 0):
                        dve.wait_ge(y_stored, xin_count(*last))
                    for i, (b, w0, w1) in enumerate(((6, 0, 4), (7, 4, WS))):
                        dve.wait_ge(proj_done, 2 * t + i + 1)
                        nc.vector.tensor_tensor(y_strip[:, w0:w1, :].rearrange("h w c -> h (w c)"), bk(b)[0:H, 0:C * (w1 - w0)],
                                                xres[:, w0:w1, :].rearrange("h w c -> h (w c)"), ALU.add).then_inc(y_done, 1)

                def normalise_out(t, m, b):
                    dve.wait_ge(av_done, 2 * t + m + 1)
                    av = bk(b)[0:PAIRP, 0:HP * NH * HV].rearrange("q (p h d) -> q p h d", p=HP, d=HV)
                    nc.vector.reciprocal(rc[m][0:PAIRP], av[:, :, :, HD]).then_inc(recip_done, 1)
                    dve.wait_ge(recip_done, 2 * t + m + 1)
                    nc.vector.tensor_tensor(o_norm[m][0:PAIRP], av[:, :, :, 0:HD],
                                            rc[m][0:PAIRP].unsqueeze(3).broadcast_to([PAIRP, HP, NH, HD]), ALU.mult).then_inc(on_done, 1)

                def step(n, j, prev, ahead):
                    t = n * NW + j
                    last = isinstance(j, int) and j == NW - 1
                    end_near = isinstance(j, int) and j == NW - 2
                    more = not (last and isinstance(n, int) and n == NI - 1)
                    kind = max(0, j - (NW - 3)) if isinstance(j, int) else 0
                    for i in range(NCH):
                        add_bias(t, i, kind)
                        row_max(t, i)
                        if prev and i == 0:
                            normalise_out(t - 1, 1, 7)
                    dve.wait_ge(v_done, t + 1)
                    src = bank3[PAD:PAIRP, :, 0:HP * C].rearrange("k b (p c) -> k b p c", c=C)
                    odd = v01[:, :, :].rearrange("k (b p a) c -> k a b p c", b=2, a=2)
                    nc.vector.tensor_copy(odd[0:TOK, 1, :, :, 0:HD], src[:, :, :, 0:HD]).then_inc(v_evac_dve, 1)
                    nc.vector.tensor_copy(odd[PAD:PAIRP, 1, :, :, HV:HV + HD], src[:, :, :, HD:2 * HD]).then_inc(v_evac_dve, 1)
                    src2 = bank3[PAD:PAIRP, :, 0:HP * C].rearrange("k b (g o c) -> k o b g c", o=2, c=C)
                    dst2 = v2[:, :, :, :, :].rearrange("k (b g) a o c -> k a o b g c", b=2)
                    nc.vector.tensor_copy(dst2[0:TOK, 1, 0, :, :, 0:HD], src2[:, 0, :, :, 2 * HD:C]).then_inc(v_evac_dve, 1)
                    nc.vector.tensor_copy(dst2[PAD:PAIRP, 1, 1, :, :, 0:HD], src2[:, 1, :, :, 2 * HD:C]).then_inc(v_evac_dve, 1)
                    if prev:
                        residual(t - 1, *before(n, j))
                    if more:
                        move_queries(t + 1)
                    if ahead:
                        x_statistics(t + NW + 1, ahead_of(n, j)[1])
                    if end_near:
                        channel_statistics(n + 1, (n + 2) * NW, ahead)
                    if more:
                        move_keys(t + 1)
                    if end_near:
                        channel_spread(n + 1)
                    normalise_out(t, 0, 7)
                    if end_near:
                        group_variance(n + 1)
                    if prev:
                        y_statistics(t - 1, j)
                    if end_near:
                        scale_and_shift(n + 1)
                        broadcast_y_statistics(n + 1)
                    if last:
                        keep_y_statistics(n + 1, t)

                def before(n, j):
                    if isinstance(j, int) and j == 0:
                        return (n - 1, NW - 2), (n - 1, NW - 1)
                    return (n, j - 2), (n, j - 1)

                move_queries(0)
                move_keys(0)
                walk(dve, step)
                normalise_out(NI * NW - 1, 1, 7)
                residual(NI * NW - 1, *before(NI, 0))
                y_statistics(NI * NW - 1, 0)
                dve.wait_ge(y_stats, 2 * NI * NW)
                all_statistics(NI + 1, None, NI * NW, False)

            @block.tensor
            def _(pe):
                pe.wait_ge(psum_ready, 8)
                pe.wait_ge(consts_in, 16 * 11)
                nc.tensor.matmul(bk(7)[C:C + 1, 0:C], b_qkv[:, 2:3], w_proj[0:C, :], start=True, stop=True).then_inc(setup_mm, 1)

                def transposes(strip, done):
                    for w in range(WS):
                        b, at = (3, w) if w < 4 else (4, w - 4)
                        mm = nc.tensor.transpose(bk(b)[0:C, H * at:H * at + H], strip[:, w, :], ident[0:H, 0:H])
                        if w in (3, WS - 1):
                            mm.then_inc(done, 1)

                def transpose_x(n, j):
                    pe.wait_ge(xin_loaded, xin_count(n, j))
                    transposes(xin, xT_done)

                def queries(t):
                    pe.wait_ge(xn_done, t + 1)
                    for i in range(2):
                        nc.tensor.matmul(q_bank(i)[0:C, 0:HS], w_qkv[:, 0:C], xn[:, NP * i:NP * i + NP, 0:TOK],
                                         start=True, stop=True).then_inc(qk_done, 1)

                def keys(s=None):
                    for i in range(2):
                        if s is not None:
                            pe.wait_ge(xT_evac, 2 * s + i + 1)
                        nc.tensor.matmul(bk(3 + i)[0:C, 0:HS], w_qkv[:, C:2 * C], xn[:, NP * i:NP * i + NP, 0:TOK],
                                         start=True, stop=True).then_inc(qk_done, 1)

                def scores(i):
                    p0, p1 = CHUNKS[i]
                    for w in range(2 * p0, 2 * p1):
                        a, at = w % 2, NH * TOK * (w // 2 - p0)
                        mm = nc.tensor.matmul(ps_scores[PAD * a:PAD * a + TOK, i, at:at + NH * TOK],
                                              q_sb[:, TOK * w:TOK * w + TOK],
                                              k_sb[:, w, :, :].rearrange("c h k -> c (h k)"), start=True, stop=True)
                    mm.then_inc(scores_done, 1)

                def values():
                    for p in range(NP):
                        mm = nc.tensor.matmul(bank3[0:PAIRP, p // HP, C * (p % HP):C * (p % HP) + C],
                                              xn[:, 2 * p:2 * p + 2, :].rearrange("c a k -> c (a k)")[:, 0:PAIRP],
                                              w_qkv[:, 2 * C:3 * C], start=True, stop=True)
                    mm.then_inc(v_done, 1)

                def transpose_p(m, first=0, end=HP):
                    for p in range(first, end):
                        mm = nc.tensor.transpose(bk(5)[0:PAIRP, 128 * p:128 * p + PAIRP],
                                                 p01[0:PAIRP, HP * m + p, :, :].rearrange("q a k -> q (a k)")[:, 0:PAIRP], ident[0:PAIRP, 0:PAIRP])
                    if end == HP:
                        mm.then_inc(pt_done, 1)

                def transpose_p2(m):
                    for g in range(HP // 2):
                        mm = nc.tensor.transpose(bk(6)[0:PAIRP, 128 * g:128 * g + PAIRP],
                                                 p2[0:PAIRP, HP * m + 2 * g:HP * m + 2 * g + 2, :].rearrange("q a k -> q (a k)")[:, 0:PAIRP], ident[0:PAIRP, 0:PAIRP])
                    mm.then_inc(pt_done, 1)

                def weighted_values(m, b):
                    av = bk(b)[:, 0:HP * NH * HV].rearrange("q (p d) -> q p d", p=HP)
                    for p in range(HP):
                        for a in range(2):
                            w = 2 * (HP * m + p) + a
                            rows = slice(PAD * a, PAD * a + TOK)
                            mm = nc.tensor.matmul(av[rows, p, 0:2 * HV], pt01[0:PAIRP, p, a, :], v01[0:PAIRP, w, :], start=True, stop=True)
                            if p % 2:
                                mm = nc.tensor.matmul(av[rows, p - 1:p + 1, 2 * HV:3 * HV], pt2[0:PAIRP, p // 2, a, :],
                                                      v2[0:PAIRP, (HP * m + p) // 2, a, :, :].rearrange("k o c -> k (o c)"), start=True, stop=True)
                    mm.then_inc(av_done, 1)

                def transpose_o(m, b):
                    for p in range(HP):
                        mm = nc.tensor.transpose(bk(b)[0:C, 128 * p:128 * p + PAIRP],
                                                 o_norm[m][0:PAIRP, p, :, :].rearrange("q h d -> q (h d)"), ident[0:PAIRP, 0:PAIRP])
                    mm.then_inc(ot_done, 1)

                def project():
                    for w in range(WS):
                        b, at = (6, w) if w < 4 else (7, w - 4)
                        mm = nc.tensor.matmul(bk(b)[0:H, C * at:C * at + C], oT[:, w, :, :].rearrange("c i h -> c (i h)"), w_proj[:, :], start=True, stop=True)
                        if w in (3, WS - 1):
                            mm.then_inc(proj_done, 1)

                def group_means(i):
                    pe.wait_ge(agg_dve, 3 * i + 1)
                    nc.tensor.matmul(ps_scores[0:C, 0, 500:502], group_sb[:, :], mv[:, :, 0], start=True, stop=True).then_inc(agg_pe, 1)

                def group_spreads(i):
                    pe.wait_ge(agg_dve, 3 * i + 2)
                    nc.tensor.matmul(ps_scores[0:C, 0, 504:506], group_sb[:, :], spread[:, :], start=True, stop=True).then_inc(agg_pe, 1)

                def row_forms(i):
                    pe.wait_ge(agg_copy, 7 * i + 6)
                    for s in range(3):
                        mm = nc.tensor.matmul(ps_scores[:, 0, C * s:C * s + C], stat_bc[:, s, :], ident[0:C, 0:C], start=True, stop=True)
                    mm.then_inc(rows_mm, 1)

                transpose_x(0, 0)
                with pe.Fori(1, NW - 1) as j:
                    pe.wait_ge(xT_evac, 2 * j)
                    pe.wait_ge(x_stats, 2 * j)
                    transpose_x(0, j)
                pe.wait_ge(xT_evac, 2 * (NW - 1))
                pe.wait_ge(x_stats, 2 * (NW - 1))
                transpose_x(0, NW - 1)
                pe.wait_ge(xT_evac, 2 * NW)
                pe.wait_ge(x_stats, 2 * NW)
                group_means(0)
                group_spreads(0)
                pe.wait_ge(consts_ready, 2)
                pe.wait_ge(setup_pool, 15)
                transpose_x(1, 0)
                queries(0)
                keys(NW)

                def step(n, j, prev, ahead):
                    t = n * NW + j
                    last = isinstance(j, int) and j == NW - 1
                    end_near = isinstance(j, int) and j == NW - 2
                    more = not (last and isinstance(n, int) and n == NI - 1)
                    s = t + NW + 1
                    pe.wait_ge(q_evac_dve, t + 1)
                    pe.wait_ge(k_evac_act, len(ACT_KEYS) * (2 * t + 1))
                    pe.wait_ge(k_evac_dve, len(DVE_KEYS) * (2 * t + 1))
                    if prev:
                        pe.wait_ge(bias_added, NCH * t)
                    if prev and isinstance(j, int) and j == 0:
                        pe.wait_ge(rows_evac, n)
                    scores(0)
                    if prev:
                        pe.wait_ge(pt_evac, 4 * t)
                        pe.wait_ge(ot_evac, 2 * t - 1)
                        weighted_values(1, 7)
                    pe.wait_ge(q_evac_act, t + 1)
                    pe.wait_ge(k_evac_act, 2 * len(ACT_KEYS) * (t + 1))
                    pe.wait_ge(k_evac_dve, 2 * len(DVE_KEYS) * (t + 1))
                    scores(1)
                    scores(2)
                    if prev:
                        pe.wait_ge(on_done, 2 * t)
                        transpose_o(1, 5)
                    if prev and not (isinstance(t, int) and t == 1):
                        pe.wait_ge(y_stats, 2 * (t - 1))
                    values()
                    if prev:
                        pe.wait_ge(ot_evac, 2 * t)
                        project()
                    pe.wait_ge(exp_done, 2 * NCH * t + 1)
                    transpose_p(0, 0, PB)
                    pe.wait_ge(v_evac_act, 4 * (t + 1))
                    pe.wait_ge(v_evac_dve, 4 * (t + 1))
                    if ahead:
                        transpose_x(*ahead_of(n, j))
                    if prev:
                        pe.wait_ge(y_done, 2 * t)
                    pe.wait_ge(exp_done, 2 * NCH * t + 4)
                    transpose_p(0, PB)
                    transpose_p2(0)
                    pe.wait_ge(bias_added, NCH * (t + 1))
                    if last:
                        row_forms(n + 1)
                    if more:
                        queries(t + 1)
                        keys(s if ahead else None)
                    pe.wait_ge(pt_evac, 4 * t + 2)
                    weighted_values(0, 7)
                    if end_near:
                        group_means(n + 1)
                    pe.wait_ge(exp_done, 2 * NCH * (t + 1))
                    transpose_p(1)
                    transpose_p2(1)
                    if end_near:
                        group_spreads(n + 1)
                    if more:
                        pe.wait_ge(k_evac_act, 2 * len(ACT_KEYS) * (t + 2))
                        pe.wait_ge(k_evac_dve, 2 * len(DVE_KEYS) * (t + 2))
                    if prev:
                        transposes(y_strip, yT_done)
                    pe.wait_ge(on_done, 2 * t + 1)
                    transpose_o(0, 7)
                    if end_near:
                        pe.wait_ge(agg_dve, 3 * (n + 2))

                walk(pe, step)
                t = NI * NW
                pe.wait_ge(pt_evac, 4 * t)
                pe.wait_ge(ot_evac, 2 * t - 1)
                weighted_values(1, 7)
                pe.wait_ge(on_done, 2 * t)
                transpose_o(1, 5)
                pe.wait_ge(ot_evac, 2 * t)
                project()
                pe.wait_ge(y_done, 2 * t)
                transposes(y_strip, yT_done)
                pe.wait_ge(rows_evac, NI)
                group_means(NI + 1)
                group_spreads(NI + 1)
                row_forms(NI + 1)

        phase_c = ExitStack()
        with phase_c:
            band = phase_c.enter_context(nc.sbuf_tensor("band", [128, 2, C, 128], F32))
            y_img = [phase_c.enter_context(nc.sbuf_tensor(f"y_img{u}", [128, BLK * C], F32)) for u in range(2)]
            rows = [phase_c.enter_context(nc.sbuf_tensor(f"rows{u}", [128, 3, C], F32)) for u in range(2)]
            z = [phase_c.enter_context(nc.sbuf_tensor(f"z{u}", [128, CG, BLK], F32)) for u in range(2)]
            v = [phase_c.enter_context(nc.sbuf_tensor(f"v{u}", [128, CG, OUTB], F32)) for u in range(2)]

            POOL_ADDS = [g for g in range(NCG) if g % 3]
            DVE_ADDS = [g for g in range(NCG) if g % 3 == 0]
            HALVES = ((slice(64, 128), 0), (slice(0, 64), NWB))
            MC = 64
            BANKS = 4

            def conv_bank(g):
                return (bk(3), bk(4), bk(5), bk(6))[g % BANKS]

            block = phase_c.enter_context(nc.Block())

            @block.sync
            def _(sp):
                for i in range(4):
                    if i >= 2:
                        sp.wait_ge(band_copied[i % 2], i // 2)
                    sp.dma_start(y_img[i % 2][:, 0:MC * C],
                                 band_dram[i // 2, :, MC * (i % 2):MC * (i % 2) + MC, :].rearrange("p m c -> p (m c)")
                                 ).then_inc(band_in[i % 2], 16)

                def load(n, u):
                    sp.dma_start(rows[u][:, :, :].rearrange("p s c -> p (s c)"),
                                 rows_dram[bass.ds(n + 1, 1), :, :].rearrange("a p c -> (a p) c")).then_inc(y_in[u], 16)
                    img = y_img[u][:, :].rearrange("p (b w c) -> p b w c", w=NWB, c=C)
                    for r in range(PR):
                        for wb in range(NWB):
                            sp.dma_start(img[PC * r:PC * r + PC, :, wb, :],
                                         y_pad[bass.ds(n + 1, 1), r::PR, OC * wb:OC * wb + PC, :].rearrange("a b w c -> w (a b) c")
                                         ).then_inc(y_in[u], 16)

                def store(n, u):
                    img = y_img[u][:, :].rearrange("p (b w c) -> p b w c", w=NWB, c=C)
                    for r in range(PR):
                        row = (r + PR - HALO) % PR
                        b0 = 0 if r >= HALO else 1
                        for wb in range(NWB):
                            sp.dma_start(out[bass.ds(n, 1), row::PR, OC * wb:OC * wb + OC, :].rearrange("a b w c -> w (a b) c"),
                                         img[PC * r + HALO:PC * r + HALO + OC, b0:b0 + NB, wb, :]).then_inc(out_stored, 16)

                for u in range(2):
                    sp.wait_ge(band_copied[u], 2)
                    load(u, u)

                def finish(n, u):
                    sp.wait_ge(added_dve, len(DVE_ADDS) * 2 * (n + 1))
                    sp.wait_ge(added_pool, 2 + len(POOL_ADDS) * 2 * (n + 1))
                    store(n, u)

                with sp.Fori(0, NI // 2 - 1) as k:
                    for u in range(2):
                        n = 2 * k + u
                        finish(n, u)
                        sp.wait_ge(out_stored, 16 * PR * NWB * (n + 1))
                        load(n + 2, u)
                for u in range(2):
                    finish(NI - 2 + u, u)
                sp.wait_ge(out_stored, 16 * PR * NWB * NI)

            @block.scalar
            def _(act):
                for i in (0, 2):
                    act.wait_ge(band_in[0], 16 * (i // 2 + 1))
                    nc.scalar.activation(band[:, i // 2, :, 0:MC], y_img[0][:, 0:MC * C].rearrange("p (m c) -> p c m", c=C),
                                         ACT.Copy, scale=alpha_col).then_inc(band_copied[0], 1)

                def step(n, u):
                    act.wait_ge(y_in[u], 16 * (1 + PR * NWB) * (k_of(n, u) + 1))
                    img = y_img[u][:, :].rearrange("p (b c) -> p c b", c=C)
                    for g in range(NCG):
                        act.wait_ge(gated, 2 * BANKS + 2 * (NCG * n + g - 1))
                        for i in range(CG):
                            c = CG * g + i
                            zz = nc.scalar.activation(z[g % 2][:, i, :], img[:, c, :], ACT.Identity,
                                                      bias=rows[u][:, 2, c:c + 1], scale=rows[u][:, 1, c:c + 1])
                        zz.then_inc(z_ready, 1)

                with act.Fori(0, NI // 2) as k:
                    def k_of(n, u):
                        return k
                    for u in range(2):
                        step(2 * k + u, u)

            @block.tensor
            def _(pe):
                pe.wait_ge(band_copied[0], 2)
                pe.wait_ge(band_copied[1], 2)
                with pe.Fori(0, NI // 2) as k:
                    for u in range(2):
                        n = 2 * k + u
                        for g in range(NCG):
                            pe.wait_ge(z_ready, NCG * n + g + 1)
                            pe.wait_ge(gated, 2 * (NCG * n + g) + 2)
                            for i in range(CG):
                                o = conv_bank(g)[:, OUTB * i:OUTB * i + OUTB]
                                nc.tensor.matmul(o, band[:, 0, CG * g + i, :], z[g % 2][:, i, 0:OUTB], start=True, stop=False)
                                mm = nc.tensor.matmul(o, band[:, 1, CG * g + i, :], z[g % 2][:, i, NWB:NWB + OUTB], start=False, stop=True)
                            mm.then_inc(conv_done, 1)

            def add_group(engine, u, g, done):
                img = y_img[u][:, :].rearrange("p (b c) -> p c b", c=C)
                for rows_, b0 in HALVES:
                    part = img[rows_, CG * g:CG * g + CG, b0:b0 + OUTB]
                    engine.tensor_tensor(part, v[g % 2][rows_, :, :], part, ALU.add).then_inc(done, 1)

            @block.vector
            def _(dve):
                for i in (1, 3):
                    dve.wait_ge(band_in[1], 16 * (i // 2 + 1))
                    nc.vector.tensor_scalar(band[:, i // 2, :, MC:2 * MC], y_img[1][:, 0:MC * C].rearrange("p (m c) -> p c m", c=C),
                                            alpha_col, None, ALU.mult).then_inc(band_copied[1], 1)
                for g in range(BANKS):
                    nc.vector.memset(conv_bank(g)[:, :], 0.0).then_inc(gated, 2)
                with dve.Fori(0, NI // 2) as k:
                    for u in range(2):
                        n = 2 * k + u
                        for g in range(NCG):
                            dve.wait_ge(conv_done, NCG * n + g + 1)
                            dve.wait_ge(added_pool, 2 + 2 * (len(POOL_ADDS) * n + len([q for q in POOL_ADDS if q <= g - 2])))
                            if g - 2 in DVE_ADDS:
                                dve.wait_ge(added_dve, 2 * (len(DVE_ADDS) * n + len([q for q in DVE_ADDS if q <= g - 2])))
                            for rows_, b0 in HALVES:
                                nc.vector.scalar_tensor_tensor(
                                    v[g % 2][rows_, :, :], conv_bank(g)[rows_, 0:CG * OUTB].rearrange("p (c b) -> p c b", c=CG),
                                    gate_one[rows_, :], z[g % 2][rows_, :, b0:b0 + OUTB], ALU.add, ALU.mult).then_inc(gated, 1)
                            if g in DVE_ADDS:
                                dve.wait_ge(gated, 2 * BANKS + 2 * (NCG * n + g + 1))
                                add_group(nc.vector, u, g, added_dve)

            @block.gpsimd
            def _(pool):
                for q in range(2):
                    nc.gpsimd.memset(v[q][:, :, :], 0.0).then_inc(added_pool, 1)
                with pool.Fori(0, NI // 2) as k:
                    for u in range(2):
                        n = 2 * k + u
                        for g in POOL_ADDS:
                            pool.wait_ge(gated, 2 * BANKS + 2 * (NCG * n + g + 1))
                            add_group(nc.gpsimd, u, g, added_pool)


def host_bias_windows(table):
    import numpy as np
    flipped = table.reshape(2 * WS - 1, 2 * WS - 1, NH)[::-1, ::-1]
    last = WS - 1
    win = [flipped[last - h:last - h + WS, last - w:last - w + WS].transpose(2, 1, 0).reshape(NH, TOK)
           for w in range(WS) for h in range(WS)]
    return np.stack(win)


def host_masks():
    import numpy as np
    side = np.repeat([0, 1, 2], [H - WS, WS - SS, SS])
    side = np.roll(side, -SS).reshape(NW, WS)
    m = np.zeros((PAIRP, 3, 2, TOK), np.float32)
    for k, column in enumerate((0, NW - 2, NW - 1)):
        for i, (upper, lower) in enumerate(((0, 1), (NW - 2, NW - 1))):
            for start, row in ((0, upper), (PAD, lower)):
                region = (side[column][:, None] + 3 * side[row][None, :]).reshape(TOK)
                m[start:start + TOK, k, i] = np.where(region[:, None] != region[None, :], np.float32(-1e9), np.float32(0))
    return m


def kernel(x, L0_conv_qkv_w, L0_conv_qkv_b, L0_conv_proj_w, L0_conv_proj_b, L0_conv_bias_table,
           L1_conv_kernel, L1_conv_alpha, L1_conv_bias):
    import numpy as np
    import concourse.bacc as bacc
    from concourse.bass_utils import run_bass_kernel_spmd

    nc = bacc.Bacc("TRN2", target_bir_lowering=False, num_devices=1)
    arrays = {
        "x": x,
        "qkv_w": L0_conv_qkv_w,
        "qkv_b": np.asarray(L0_conv_qkv_b).reshape(3, C).T,
        "proj_w": L0_conv_proj_w,
        "proj_b": np.asarray(L0_conv_proj_b).reshape(1, C),
        "bias_win": host_bias_windows(np.asarray(L0_conv_bias_table)),
        "taps": L1_conv_kernel,
        "alpha": L1_conv_alpha,
        "bias": L1_conv_bias,
        "masks": host_masks(),
        "eye": np.eye(128, dtype=np.float32),
        "group": np.kron(np.eye(C // 3, dtype=np.float32), np.full((3, 3), 1 / 3, np.float32)),
    }
    arrays = {f"in_{k}": np.ascontiguousarray(a) for k, a in arrays.items()}
    aps = [nc.dram_tensor(k, a.shape, F32, kind="ExternalInput").ap() for k, a in arrays.items()]
    out = nc.dram_tensor("out", (NI, H, W, C), F32, kind="ExternalOutput").ap()
    attention_then_conv(nc, *aps, out)
    return run_bass_kernel_spmd(nc, [arrays], core_ids=[0]).results[0]["out"]
```

```python
from contextlib import ExitStack

import concourse.bass as bass
from concourse import mybir

F32 = mybir.dt.float32
ALU = mybir.AluOpType
ACT = mybir.ActivationFunctionType
AX_X = mybir.AxisListType.X

NI, H, W, C = 32, 112, 112, 96
WS, SS, NH = 7, 3, 3
HD = C // NH
NW = H // WS
TOK = WS * WS
PAD = 64
PAIRP = PAD + TOK
STRIP = NW * TOK
NP = NW // 2
PB = 512 // (NH * TOK)
CHUNKS = [(p, min(p + PB, NP)) for p in range(0, NP, PB)]
NCH = len(CHUNKS)
HP = NP // 2
HS = STRIP // 2
HV = HD + 1
SCALE = float(HD) ** -0.5
EPS = 1e-5
KS = 5
HALO = KS // 2
BORDER = 1 + 8 + 12
N_BAND = KS * 4
PR, PC = 4, 32
OC = PC - KS + 1
NB, NWB = H // PR, W // OC
HB, WP = H + KS - 1, W + KS - 1
BLK = (NB + 1) * NWB
OUTB = NB * NWB
CG = 4
NCG = C // CG
ROWS = 3 * C
ROW_CUTS = [(0, SS, 96), (96, SS + 96, H - SS - 96), (H - SS, 0, SS)]


ROW_PIECES = PR + 2


def patch_columns(j):
    at = WS * j + SS + HALO
    v, w = at // OC, at % OC
    if j == NW - 1:
        own = W - WS * j - SS
        return [(0, own, at - OC * (NWB - 1), NWB - 1), (own, SS, HALO, 0)]
    if w + WS <= OC:
        return [(0, WS, w, v)]
    own = PC - w
    return [(0, own, w, v), (OC - w, WS - (OC - w), 0, v + 1)]


def attention_then_conv(nc, x, qkv_w, qkv_b, proj_w, proj_b, bias_win, taps, alpha, bias, masks, eye, group, out):
    y_patch = nc.dram_tensor("y_patch", (NI + 1, PR, PC, NB + 1, NWB, C), F32, kind="Internal").ap()
    rows_dram = nc.dram_tensor("rows_dram", (NI + 1, 128, ROWS), F32, kind="Internal").ap()
    band_dram = nc.dram_tensor("band_dram", (2, 128, 128, C), F32, kind="Internal").ap()

    ctx = ExitStack()
    with ctx:
        def sb(name, shape, space=ctx):
            return space.enter_context(nc.sbuf_tensor(name, shape, F32))

        def sem(name):
            return ctx.enter_context(nc.semaphore(name))

        ps_scores = ctx.enter_context(nc.psum_tensor("ps_scores", [128, NCH, 512], F32))
        bank3 = ctx.enter_context(nc.psum_tensor("bank34", [128, 2, 512], F32))
        bank = {b: ctx.enter_context(nc.psum_tensor(f"bank{b}", [128, 512], F32)) for b in (5, 6, 7)}

        def q_bank(i):
            return ps_scores[:, 1 + i, :]

        def bk(b):
            return bank3[:, b - 3, :] if b < 5 else bank[b][:, :]

        ident = sb("ident", [128, 128])
        small = sb("small", [128, 16])
        alpha_col, gate_one = small[:, 0:1], small[:, 1:2]

        consts_in, consts_ready, zeros_ready, psum_ready = sem("consts_in"), sem("consts_ready"), sem("zeros_ready"), sem("psum_ready")
        setup_mm, setup_dve, setup_pool = sem("setup_mm"), sem("setup_dve"), sem("setup_pool")
        band_zeroed, band_written = sem("band_zeroed"), sem("band_written")
        first_loaded = [sem("first_loaded0"), sem("first_loaded1"), sem("first_loaded2")]
        xin_loaded, xres_loaded, y_stored = sem("xin_loaded"), sem("xres_loaded"), [sem("y_stored_even"), sem("y_stored_odd")]
        xT_done, xT_evac_act, xT_evac_dve, x_stats = sem("xT_done"), sem("xT_evac_act"), sem("xT_evac_dve"), sem("x_stats")
        xn_done, qk_done, q_evac, k_evac_act, k_evac_dve = (
            sem("xn_done"), sem("qk_done"), sem("q_evac"), sem("k_evac_act"), sem("k_evac_dve"))
        v_done, v_evac_act, v_evac_dve = sem("v_done"), sem("v_evac_act"), sem("v_evac_dve")
        scores_done, bias_added, max_done, sub_done, exp_done = (
            sem("scores_done"), sem("bias_added"), sem("max_done"), sem("sub_done"), sem("exp_done"))
        pt_done, pt_evac, av_done, recip_done, on_done = (
            sem("pt_done"), sem("pt_evac"), sem("av_done"), sem("recip_done"), sem("on_done"))
        ot_done, ot_evac, proj_done, y_done, yT_done, y_stats = (
            sem("ot_done"), sem("ot_evac"), sem("proj_done"), sem("y_done"), sem("yT_done"), sem("y_stats"))
        agg_dve, agg_pe, agg_pool, norm_ready, bc_ready = (
            sem("agg_dve"), sem("agg_pe"), sem("agg_pool"), sem("norm_ready"), sem("bc_ready"))
        agg_copy = sem("agg_copy")
        rows_mm, rows_evac, rows_stored = sem("rows_mm"), sem("rows_evac"), sem("rows_stored")
        band_in, band_copied = [sem("band_in0"), sem("band_in1")], [sem("band_copied0"), sem("band_copied1")]
        y_in = [sem("y_in0"), sem("y_in1")]
        z_ready, conv_done, gated, added_dve, added_pool, out_stored = (
            sem("z_ready"), sem("conv_done"), sem("gated"), sem("added_dve"), sem("added_pool"),
            [sem(f"out_stored{r}") for r in range(PR)])

        phase_b = ExitStack()
        with phase_b:
            def sbb(name, shape):
                return sb(name, shape, phase_b)

            xT = sbb("xT", [C, NW, NW, WS, WS])
            xin = sbb("xin", [H, WS, C])
            xres = sbb("xres", [H, WS, C])
            y_strip = [sbb(f"y_strip{u}", [H, WS, C]) for u in range(2)]
            xn = sbb("xn", [C, NW, PAD])
            q_sb = sbb("q_sb", [C, STRIP])
            k_sb = sbb("k_sb", [C, NW, NH, TOK])
            v01 = sbb("v01", [128, NW, 2 * HV])
            v2 = sbb("v2", [128, HP, 2, 2, HV])
            t_sb = sbb("t_sb", [128, NP, NH, TOK])
            mx = sbb("mx", [128, NP, NH])
            p01 = sbb("p01", [128, NP, 2, PAD])
            p2 = sbb("p2", [128, NP, PAD])
            pt01 = sbb("pt01", [128, HP, 2, TOK])
            pt2 = sbb("pt2", [128, HP // 2, 2, TOK])
            rc = [sbb(f"rc{m}", [128, HP, NH]) for m in range(2)]
            o_norm = [sbb(f"o_norm{m}", [128, HP, NH, HD]) for m in range(2)]
            oT = sbb("oT", [C + 1, WS, NW, WS])
            bias_sb = sbb("bias_sb", [128, 3, NP, NH, TOK])
            bias_base = sbb("bias_base", [128, NH, TOK])
            mask_sb = sbb("mask_sb", [128, 3, 2, TOK])
            w_qkv = sbb("w_qkv", [C, 3 * C])
            w_proj = sbb("w_proj", [C + 1, C])
            b_qkv = sbb("b_qkv", [C, 3])
            b_keys = sbb("b_keys", [128, 2, 3])
            b_proj = sbb("b_proj", [C + 1, C])
            group_sb = sbb("group_sb", [C, C])
            x_bn = sbb("x_bn", [C, NW, 2, 6])
            y_bn = sbb("y_bn", [C, NW, 2, 6])
            y_agg_in = sbb("y_agg_in", [C, NW, 2, 6])
            mv = sbb("mv", [C, 2, 2])
            dev = sbb("dev", [C, 2])
            spread = sbb("spread", [C, 2])
            var_eps = sbb("var_eps", [C, 2])
            carrier = sbb("carrier", [C, 1])
            minus_half = sbb("minus_half", [C, 2])
            stat = sbb("stat", [C, 3, 2])
            stat_bc = sbb("stat_bc", [C, 3, 128])
            rows_sb = sbb("rows_sb", [128, ROWS])
            zeros = sbb("zeros", [128, 16 * C])

            b_q_scaled = small[0:C, 2:3]
            def xin_count(n, j):
                return 16 * len(ROW_CUTS) * ((NW + 1) * n + j + 1) + (16 * len(ROW_CUTS) if isinstance(j, int) and j == NW - 1 else 0)

            def xin_ahead(n, j):
                return xin_count(n, j) - 16 * len(ROW_CUTS) * (NW + 2)

            first_in = (y_strip[0], xin, xres)

            def y_count(n, j, u):
                if u == 0:
                    return 16 * ROW_PIECES * (NW // 2 * n + (j >> 1) + 1)
                return 16 * ROW_PIECES * ((NW // 2 + NW // 4) * n + ((j + 1) >> 1) + ((j + 1) >> 2))

            ACT_KEYS, DVE_KEYS = (0, 1), (2,)
            QK0 = C + HD

            def key_block(i, h):
                if h == 0:
                    rows_, b, column = slice(C, QK0), q_bank(i), 0
                else:
                    low = (PAD if i else 0) + HD * (h - 1)
                    rows_, b, column = slice(low, low + HD), bk(3 + i), 1
                return (b[rows_, 0:HS].rearrange("c (w k) -> c w k", k=TOK), b_keys[rows_, column, 1:2],
                        k_sb[HD * h:HD * h + HD, NP * i:NP * i + NP, h, :])

            block = phase_b.enter_context(nc.Block())

            def walk(eng, step):
                def image(n, prev, ahead, last_ahead):
                    first = 2 if prev else 4
                    for j in range(first):
                        step(n, j, j % 2, prev or j > 0, ahead)
                    with eng.Fori(first // 2, NW // 2 - 1) as k:
                        for u in range(2):
                            step(n, 2 * k + u, u, True, ahead)
                    step(n, NW - 2, 0, True, ahead)
                    step(n, NW - 1, 1, True, last_ahead)

                image(0, False, True, True)
                with eng.Fori(1, NI - 2) as n:
                    image(n, True, True, True)
                image(NI - 2, True, True, False)
                image(NI - 1, True, False, False)

            def xT_half(slot, b):
                w0, w1 = ((0, 4), (4, WS))[b]
                return (bk(3 + b)[0:C, 0:H * (w1 - w0)].rearrange("c (w i h) -> c w i h", i=NW, h=WS),
                        xT[:, bass.ds(slot, 1), :, w0:w1, :].rearrange("c a i w h -> c w (a i) h"))

            def ahead_of(n, j):
                if isinstance(j, int) and j == NW - 1:
                    return n + 2, 0
                return n + 1, j + 1

            @block.sync
            def _(sp):
                sp.dma_start(ident[:, :], eye).then_inc(consts_in, 16)
                sp.dma_start(w_qkv[:, :], qkv_w).then_inc(consts_in, 16)
                sp.dma_start(w_proj[0:C, :], proj_w).then_inc(consts_in, 16)
                sp.dma_start(b_qkv[:, :], qkv_b).then_inc(consts_in, 16)
                sp.dma_start(b_proj[C:C + 1, :], proj_b).then_inc(consts_in, 16)
                sp.dma_start(b_keys[C:QK0, 0, :], qkv_b[0:HD, :]).then_inc(consts_in, 16)
                for lo in (0, PAD):
                    sp.dma_start(b_keys[lo:lo + C - HD, 1, :], qkv_b[HD:C, :]).then_inc(consts_in, 16)
                for lo in (0, PAD):
                    if lo == 0:
                        sp.wait_ge(zeros_ready, 1)
                    sp.dma_start(bias_base[lo:lo + TOK, :, :], bias_win).then_inc(consts_in, 16)
                sp.dma_start(mask_sb[0:PAIRP, :, :, :], masks).then_inc(consts_in, 16)
                sp.dma_start(group_sb[:, :], group).then_inc(consts_in, 16)
                sp.dma_start(alpha_col, alpha.broadcast_to([128, 1])).then_inc(consts_in, 16)
                sp.dma_start(gate_one, bias.broadcast_to([128, 1])).then_inc(consts_in, 16)

                def column_cuts(j):
                    if isinstance(j, int) and j == NW - 1:
                        return [(0, WS * j + SS, W - WS * j - SS), (W - WS * j - SS, 0, SS)]
                    return [(0, WS * j + SS, WS)]

                def load(dst, n, j, done):
                    for p0, r0, nr in ROW_CUTS:
                        for w0, c0, ncol in column_cuts(j):
                            sp.dma_start(dst[p0:p0 + nr, w0:w0 + ncol, :],
                                         x[bass.ds(n, 1), r0:r0 + nr, bass.ds(c0, ncol), :].rearrange("a r w c -> (a r) w c")
                                         ).then_inc(done, 16)

                def store(n, q, group=0):
                    top = SS + HALO
                    unwrapped = H - SS
                    for w0, ncol, w, v in patch_columns(q):
                        image = y_patch[bass.ds(n + 1, 1), :, w:w + ncol, :, bass.ds(v + group, 1), :]
                        for p in range(PR):
                            k, b = (unwrapped - p + PR - 1) // PR, (p + top) // PR
                            sp.dma_start(image[:, (p + top) % PR, :, b:b + k, :, :].rearrange("a w b v c -> (a b) w (v c)"),
                                         y_strip[q % 2][p:unwrapped:PR, w0:w0 + ncol, :]).then_inc(y_stored[q % 2], 16)
                        sp.dma_start(image[:, HALO:PR, :, 0, :, :].rearrange("a r w v c -> (a r) w (v c)"),
                                     y_strip[q % 2][unwrapped:unwrapped + PR - HALO, w0:w0 + ncol, :]).then_inc(y_stored[q % 2], 16)
                        sp.dma_start(image[:, 0:HALO + SS - PR, :, 1, :, :].rearrange("a r w v c -> (a r) w (v c)"),
                                     y_strip[q % 2][unwrapped + PR - HALO:H, w0:w0 + ncol, :]).then_inc(y_stored[q % 2], 16)

                def stage(n, q, prev, ahead, group=0):
                    j = 4 * group + q
                    t = n * NW + j
                    if prev:
                        sp.wait_ge(y_done, 2 * t)
                    load(xres, n, j, xres_loaded)
                    if ahead:
                        sp.wait_ge(xT_done, 2 * (t + NW + 2))
                        if isinstance(j, int) and j >= NW - 2:
                            load(xin, n + 2, j - (NW - 2), xin_loaded)
                        else:
                            load(xin, n + 1, j + 2, xin_loaded)
                    if prev:
                        if isinstance(j, int) and j == 0:
                            store(n - 1, NW - 1)
                        elif isinstance(group, int):
                            store(n, j - 1)
                        elif q == 0:
                            store(n, 3, group - 1)
                        else:
                            store(n, q - 1, group)
                    if isinstance(group, int) and group == 0 and q < PR and not (isinstance(n, int) and n == 0):
                        save_rows(n - 1, q)

                def save_rows(n, r):
                    if r == 0:
                        sp.wait_ge(rows_evac, n + 1)
                        sp.dma_start(rows_dram[bass.ds(n, 1), :, :].rearrange("a p c -> (a p) c"), rows_sb[:, :]).then_inc(rows_stored, 16)
                    image = y_patch[bass.ds(n, 1), :, :, :, :, :]
                    for w, v in ((0, 0), (PC - HALO, NWB - 1)):
                        sp.dma_start(image[:, r, w:w + HALO, :, v, :].rearrange("a w b c -> (a b) w c"),
                                     rows_sb[0:NB + 1, 0:C].unsqueeze(1).broadcast_to([NB + 1, HALO, C])).then_inc(rows_stored, 16)
                    b = 0 if r < HALO else NB
                    for w0, w1, v0, v1 in ((HALO, PC - HALO, 0, NWB), (0, HALO, 1, NWB), (PC - HALO, PC, 0, NWB - 1)):
                        sp.dma_start(image[:, r, w0:w1, b, v0:v1, :].rearrange("a w v c -> (a w) v c"),
                                     rows_sb[w0:w1, 0:C].unsqueeze(1).broadcast_to([w1 - w0, v1 - v0, C])).then_inc(rows_stored, 16)

                for u in range(3):
                    load(first_in[u], 0, u, first_loaded[u])
                with sp.Fori(1, NW // 3) as k:
                    for u in range(3):
                        sp.wait_ge(xT_done, 2 * (3 * k + u - 2))
                        load(first_in[u], 0, 3 * k + u, first_loaded[u])
                sp.wait_ge(xT_done, 2 * (NW - 3))
                load(first_in[0], 0, NW - 1, first_loaded[0])
                sp.wait_ge(xT_done, 2 * (NW - 2))
                load(first_in[1], 1, 0, first_loaded[1])
                sp.wait_ge(xT_done, 2 * (NW + 1))
                load(xin, 1, 1, xin_loaded)

                def image(n, prev, ahead, last_ahead):
                    for q in range(4):
                        stage(n, q, prev or q > 0, ahead)
                    with sp.Fori(1, NW // 4 - 1) as group:
                        for q in range(4):
                            stage(n, q, True, ahead, group)
                    stage(n, NW - 4, True, ahead)
                    stage(n, NW - 3, True, ahead)
                    stage(n, NW - 2, True, last_ahead)
                    stage(n, NW - 1, True, last_ahead)

                image(0, False, True, True)
                with sp.Fori(1, NI - 2) as n:
                    image(n, True, True, True)
                image(NI - 2, True, True, False)
                image(NI - 1, True, False, False)
                for r in range(PR):
                    save_rows(NI - 1, r)
                sp.wait_ge(y_done, 2 * NI * NW)
                store(NI - 1, NW - 1)
                for r in range(PR):
                    save_rows(NI, r)
                sp.wait_ge(band_written, 16 * N_BAND)

            @block.gpsimd
            def _(pool):
                nc.gpsimd.memset(zeros[:, :], 0.0).then_inc(setup_pool, 1)
                nc.gpsimd.memset(bias_base[:, :, :], 0.0).then_inc(zeros_ready, 1)
                nc.gpsimd.memset(xn[:, :, :], 0.0).then_inc(setup_pool, 1)
                nc.gpsimd.memset(v01[:, :, :], 0.0).then_inc(setup_pool, 1)
                nc.gpsimd.memset(k_sb[:, :, :, :], 0.0).then_inc(setup_pool, 1)
                nc.gpsimd.memset(v2[:, :, :, :, :], 0.0).then_inc(setup_pool, 1)
                nc.gpsimd.memset(p01[:, :, :, :], 0.0).then_inc(setup_pool, 1)
                nc.gpsimd.memset(p2[:, :, :], 0.0).then_inc(setup_pool, 1)
                nc.gpsimd.memset(y_bn[:, :, :, :], 1.0).then_inc(setup_pool, 1)
                nc.gpsimd.memset(y_agg_in[:, :, :, :], 1.0).then_inc(setup_pool, 1)
                nc.gpsimd.memset(minus_half[:, :], -0.5).then_inc(setup_pool, 1)
                pool.wait_ge(setup_pool, 10)
                nc.gpsimd.memset(oT[C:C + 1, :, :, :], 1.0).then_inc(setup_pool, 1)
                for i, lo in enumerate((0, PAD)):
                    pool.wait_ge(setup_pool, 11 + 2 * i)
                    nc.gpsimd.memset(v01[lo:lo + PAD, :, HV * i + HD:HV * i + HV], 1.0).then_inc(setup_pool, 1)
                    pool.wait_ge(setup_pool, 12 + 2 * i)
                    nc.gpsimd.memset(v2[lo:lo + PAD, :, :, i, HD:HV], 1.0).then_inc(setup_pool, 1)
                def clear_band(pieces):
                    for piece in pieces:
                        half, g = piece // 8, piece % 8
                        pool.dma_start(band_dram[half, :, 16 * g:16 * g + 16, :].rearrange("p m c -> p (m c)"),
                                       zeros[:, :]).then_inc(band_zeroed, 16)

                def write_taps(pieces):
                    pool.wait_ge(band_zeroed, 16 * 16)
                    for piece in pieces:
                        dy, r = piece // PR, piece % PR
                        half, row = (r + dy) // PR, (r + dy) % PR
                        col = (r + KS // 2) % PR * PC + KS // 2
                        start = band_dram[half, row * PC, col, 0:1]
                        diagonals = bass.AP(band_dram.tensor, start.offset, [[128 * C, KS], [(128 + 1) * C, OC], [1, C]])
                        pool.dma_start(diagonals, taps[dy, :, :].unsqueeze(1).broadcast_to([KS, OC, C])).then_inc(band_written, 16)

                def subtract(t, i):
                    p0, p1 = CHUNKS[i]
                    pool.wait_ge(max_done, NCH * t + i + 1)
                    nc.gpsimd.tensor_tensor(t_sb[0:PAIRP, p0:p1], t_sb[0:PAIRP, p0:p1],
                                            mx[0:PAIRP, p0:p1].unsqueeze(3).broadcast_to([PAIRP, p1 - p0, NH, TOK]),
                                            ALU.subtract).then_inc(sub_done, 1)

                def power(i):
                    pool.wait_ge(agg_dve, 3 * (i + 1))
                    nc.gpsimd.tensor_tensor(stat[:, 1, :], var_eps[:, :], minus_half[:, :], ALU.pow).then_inc(agg_pool, 1)

                power(0)

                def step(n, j, u, prev, ahead):
                    t = n * NW + j
                    for i in range(NCH):
                        subtract(t, i)
                    if isinstance(j, int) and j == NW - 2:
                        power(n + 1)
                    if isinstance(n, int) and isinstance(j, int):
                        if n == 0 and j < 4:
                            clear_band(range(4 * j, 4 * j + 4))
                        for piece, place in enumerate(((0, NW - 2), (0, NW - 1), (NI - 2, 0), (NI - 2, 1))):
                            if (n, j) == place:
                                write_taps(range(KS * piece, KS * piece + KS))

                walk(pool, step)
                power(NI + 1)

            @block.scalar
            def _(act):
                act.wait_ge(consts_ready, 2)
                act.wait_ge(setup_pool, 15)

                def evac_xT(s, slot, waited=False):
                    if not waited:
                        act.wait_ge(xT_done, 2 * s + 1)
                    src, dst = xT_half(slot, 0)
                    nc.scalar.activation(dst, src, ACT.Copy).then_inc(xT_evac_act, 1)

                def normalise(t, slot, image):
                    act.wait_ge(norm_ready, image + 1)
                    act.wait_ge(xT_evac_act, t + 1)
                    act.wait_ge(xT_evac_dve, t + 1)
                    if not (isinstance(t, int) and t == 0):
                        act.wait_ge(v_done, t)
                    for i in range(2):
                        src = xT[:, bass.ds(slot, 1), NP * i:NP * i + NP, :, :].rearrange("c a i w h -> c (a i) (w h)")
                        nc.scalar.activation(xn[:, NP * i:NP * i + NP, 0:TOK], src, ACT.Identity, bias=stat[:, 2, 0:1],
                                             scale=stat[:, 1, 0:1]).then_inc(xn_done, 1)

                def evac_k(t):
                    for h in ACT_KEYS:
                        for i in range(2):
                            act.wait_ge(qk_done, 4 * t + (2 if h else 0) + i + 1)
                            src, shift, dst = key_block(i, h)
                            nc.scalar.activation(dst, src, ACT.Identity, bias=shift).then_inc(k_evac_act, 1)

                def evac_oT(t, m, b):
                    act.wait_ge(ot_done, 2 * t + m + 1)
                    src = bk(b)[0:C, :].rearrange("c (i k) -> c i k", k=PAD)[:, :, 0:TOK].rearrange("c i (w h) -> c i w h", h=WS)
                    dst = oT[0:C, :, NP * m:NP * m + NP, :].rearrange("c w i h -> c i w h")
                    nc.scalar.activation(dst, src, ACT.Copy).then_inc(ot_evac, 1)

                def exp_pair(t, i):
                    p0, p1 = CHUNKS[i]
                    act.wait_ge(sub_done, NCH * t + i + 1)
                    nc.scalar.activation(p01[0:PAIRP, p0:p1, :, 0:TOK], t_sb[0:PAIRP, p0:p1, 0:2], ACT.Exp).then_inc(exp_done, 1)

                def exp_single(t, i):
                    p0, p1 = CHUNKS[i]
                    nc.scalar.activation(p2[0:PAIRP, p0:p1, 0:TOK], t_sb[0:PAIRP, p0:p1, 2], ACT.Exp).then_inc(exp_done, 1)

                def evac_pt(t, m, i):
                    b, dst, cnt = ((5, pt01, HP), (6, pt2, HP // 2))[i]
                    act.wait_ge(pt_done, 4 * t + 2 * m + i + 1)
                    src = bk(b)[0:PAIRP, 0:128 * cnt].rearrange("k (p a q) -> k p a q", p=cnt, q=PAD)[:, :, :, 0:TOK]
                    nc.scalar.activation(dst[0:PAIRP, :, :, :], src, ACT.Copy).then_inc(pt_evac, 1)

                with act.Fori(0, NW) as j:
                    evac_xT(j, j)
                normalise(0, 0, 0)
                act.wait_ge(xn_done, 2)
                evac_xT(NW, 0)
                evac_k(0)

                def step(n, j, u, prev, ahead):
                    t = n * NW + j
                    last = isinstance(j, int) and j == NW - 1
                    exp_pair(t, 0)
                    exp_single(t, 0)
                    if prev:
                        evac_oT(t - 1, 1, 5)
                    act.wait_ge(v_done, t + 1)
                    src = bank3[0:TOK, :, 0:HP * C].rearrange("k b (p c) -> k b p c", c=C)
                    even = v01[:, :, :].rearrange("k (b p a) c -> k a b p c", b=2, a=2)
                    nc.scalar.activation(even[0:TOK, 0, :, :, 0:HD], src[:, :, :, 0:HD], ACT.Copy).then_inc(v_evac_act, 1)
                    nc.scalar.activation(even[PAD:PAIRP, 0, :, :, HV:HV + HD], src[:, :, :, HD:2 * HD], ACT.Copy).then_inc(v_evac_act, 1)
                    src2 = bank3[0:TOK, :, 0:HP * C].rearrange("k b (g o c) -> k o b g c", o=2, c=C)
                    dst2 = v2[:, :, :, :, :].rearrange("k (b g) a o c -> k a o b g c", b=2)
                    nc.scalar.activation(dst2[0:TOK, 0, 0, :, :, 0:HD], src2[:, 0, :, :, 2 * HD:C], ACT.Copy).then_inc(v_evac_act, 1)
                    nc.scalar.activation(dst2[PAD:PAIRP, 0, 1, :, :, 0:HD], src2[:, 1, :, :, 2 * HD:C], ACT.Copy).then_inc(v_evac_act, 1)
                    exp_pair(t, 1)
                    exp_single(t, 1)
                    more = not (last and isinstance(n, int) and n == NI - 1)
                    if more:
                        normalise(t + 1, 0 if last else j + 1, n + 1 if last else n)
                    exp_pair(t, 2)
                    if ahead:
                        act.wait_ge(xT_done, 2 * (t + NW + 1) + 1)
                        act.wait_ge(xn_done, 2 * (t + 2))
                    exp_single(t, 2)
                    if ahead:
                        evac_xT(t + NW + 1, ahead_of(n, j)[1], waited=True)
                    evac_pt(t, 0, 0)
                    evac_pt(t, 0, 1)
                    if last:
                        rows_out(n)
                    if more:
                        evac_k(t + 1)
                    evac_pt(t, 1, 0)
                    evac_pt(t, 1, 1)
                    evac_oT(t, 0, 7)

                def rows_out(n):
                    act.wait_ge(rows_mm, n + 1)
                    if not (isinstance(n, int) and n == 0):
                        act.wait_ge(rows_stored, 16 * BORDER * n)
                    nc.scalar.activation(rows_sb[:, :], ps_scores[:, 0, 0:ROWS], ACT.Copy).then_inc(rows_evac, 1)

                walk(act, step)
                evac_oT(NI * NW - 1, 1, 5)
                rows_out(NI)

            @block.vector
            def _(dve):
                for b in range(NCH):
                    nc.vector.memset(ps_scores[:, b, :], 1.0).then_inc(psum_ready, 1)
                for b in (3, 4, 5, 6, 7):
                    nc.vector.memset(bk(b), 1.0).then_inc(psum_ready, 1)
                dve.wait_ge(consts_in, 16 * 14)
                nc.vector.tensor_scalar(b_q_scaled, b_qkv[:, 0:1], SCALE, None, ALU.mult).then_inc(consts_ready, 1)
                nc.vector.tensor_scalar(gate_one, gate_one, 1.0, None, ALU.add).then_inc(setup_dve, 1)
                for k in range(3):
                    for p in range(NP):
                        nc.vector.tensor_tensor(bias_sb[0:PAIRP, k, p, :, :], bias_base[0:PAIRP, :, :],
                                                mask_sb[0:PAIRP, k, int(p == NP - 1), :].unsqueeze(1).broadcast_to([PAIRP, NH, TOK]),
                                                ALU.add).then_inc(setup_dve, 1)
                dve.wait_ge(setup_mm, 1)
                nc.vector.tensor_tensor(w_proj[C:C + 1, :], bk(7)[C:C + 1, 0:C], b_proj[C:C + 1, :], ALU.add).then_inc(consts_ready, 1)
                dve.wait_ge(setup_dve, 1 + 3 * NP)
                dve.wait_ge(setup_pool, 15)

                def move_xT(s, slot):
                    dve.wait_ge(xT_done, 2 * s + 2)
                    src, dst = xT_half(slot, 1)
                    nc.vector.tensor_scalar(dst, src, 1.0, None, ALU.mult).then_inc(xT_evac_dve, 1)

                def x_statistics(s, slot):
                    dve.wait_ge(xT_evac_act, s + 1)
                    dve.wait_ge(xT_evac_dve, s + 1)
                    for b in range(2):
                        nc.vector.bn_stats(x_bn[:, bass.ds(slot, 1), b, :].rearrange("c a s -> c (a s)"),
                                           xT[:, bass.ds(slot, 1), NP * b:NP * b + NP, :, :].rearrange("c a i w h -> c (a i w h)")
                                           ).then_inc(x_stats, 1)

                def y_statistics(t, slot):
                    for b, wn in enumerate((4, WS - 4)):
                        dve.wait_ge(yT_done, 2 * t + b + 1)
                        nc.vector.bn_stats(y_bn[:, bass.ds(slot, 1), b, :].rearrange("c a s -> c (a s)"),
                                           bk(3 + b)[0:C, 0:H * wn]).then_inc(y_stats, 1)

                def channel_statistics(i, s, of_x):
                    nc.vector.tensor_copy(y_agg_in[:, NW - 1, :, :], y_bn[:, 0, :, :]).then_inc(agg_copy, 1)
                    if of_x:
                        dve.wait_ge(x_stats, 2 * s)
                        nc.vector.memset(carrier[:, :], 0.0)
                    nc.vector.bn_aggr(mv[:, 0, :], x_bn[:, :, :, :].rearrange("c a b s -> c (a b s)")).then_inc(agg_copy, 1)
                    dve.wait_ge(agg_copy, 7 * i + 2)
                    nc.vector.memset(carrier[:, :], 0.0)
                    nc.vector.bn_aggr(mv[:, 1, :], y_agg_in[:, :, :, :].rearrange("c a b s -> c (a b s)")).then_inc(agg_dve, 1)

                def channel_spread(i):
                    dve.wait_ge(agg_pe, 2 * i + 1)
                    nc.vector.tensor_copy(stat[:, 0, :], ps_scores[0:C, 0, 500:502]).then_inc(agg_copy, 1)
                    nc.vector.tensor_tensor(dev[:, :], mv[:, :, 0], ps_scores[0:C, 0, 500:502], ALU.subtract).then_inc(agg_copy, 1)
                    dve.wait_ge(agg_copy, 7 * i + 4)
                    nc.vector.tensor_tensor(spread[:, :], dev[:, :], dev[:, :], ALU.mult).then_inc(agg_copy, 1)
                    dve.wait_ge(agg_copy, 7 * i + 5)
                    nc.vector.tensor_tensor(spread[:, :], spread[:, :], mv[:, :, 1], ALU.add).then_inc(agg_dve, 1)

                def group_variance(i):
                    dve.wait_ge(agg_pe, 2 * i + 2)
                    nc.vector.tensor_scalar(var_eps[:, :], ps_scores[0:C, 0, 504:506], EPS, None, ALU.add).then_inc(agg_dve, 1)

                def scale_and_shift(i):
                    dve.wait_ge(agg_pool, i + 1)
                    nc.vector.scalar_tensor_tensor(stat[:, 2, :], stat[:, 0, :], -1.0, stat[:, 1, :], ALU.mult, ALU.mult).then_inc(norm_ready, 1)

                def keep_y_statistics(i, t):
                    if t is not None:
                        dve.wait_ge(y_stats, 2 * t)
                    nc.vector.tensor_copy(y_agg_in[:, 0:NW - 1, :, :], y_bn[:, 1:NW, :, :]).then_inc(agg_copy, 1)

                def broadcast_y_statistics(i):
                    dve.wait_ge(norm_ready, i + 1)
                    nc.vector.tensor_copy(stat_bc[:, :, :], stat[:, :, 1:2].broadcast_to([C, 3, 128])).then_inc(agg_copy, 1)

                def all_statistics(i, s, t, of_x):
                    channel_statistics(i, s, of_x)
                    channel_spread(i)
                    group_variance(i)
                    scale_and_shift(i)
                    broadcast_y_statistics(i)
                    keep_y_statistics(i, t)

                with dve.Fori(0, NW) as j:
                    move_xT(j, j)
                    x_statistics(j, j)
                all_statistics(0, NW, None, True)
                dve.wait_ge(xn_done, 2)
                move_xT(NW, 0)
                x_statistics(NW, 0)

                def add_bias(t, i, kind):
                    p0, p1 = CHUNKS[i]
                    dve.wait_ge(scores_done, NCH * t + i + 1)
                    nc.vector.tensor_tensor(
                        t_sb[0:PAIRP, p0:p1].rearrange("q p h k -> q (p h k)"), ps_scores[0:PAIRP, i, 0:NH * TOK * (p1 - p0)],
                        bias_sb[0:PAIRP, kind, p0:p1].rearrange("q p h k -> q (p h k)"), ALU.add).then_inc(bias_added, 1)

                def row_max(t, i):
                    p0, p1 = CHUNKS[i]
                    dve.wait_ge(bias_added, NCH * t + i + 1)
                    nc.vector.tensor_reduce(mx[0:PAIRP, p0:p1], t_sb[0:PAIRP, p0:p1], AX_X, ALU.max).then_inc(max_done, 1)

                def move_queries(t):
                    for i in range(2):
                        dve.wait_ge(qk_done, 4 * t + i + 1)
                        nc.vector.tensor_scalar(q_sb[:, HS * i:HS * i + HS], q_bank(i)[0:C, 0:HS], SCALE, b_q_scaled,
                                                ALU.mult, ALU.add).then_inc(q_evac, 1)

                def move_keys(t):
                    for i in range(2):
                        dve.wait_ge(qk_done, 4 * t + i + 3)
                        for h in DVE_KEYS:
                            src, shift, dst = key_block(i, h)
                            nc.vector.tensor_scalar(dst, src, shift, None, ALU.add).then_inc(k_evac_dve, 1)

                def residual(t, u, last, this):
                    dve.wait_ge(xres_loaded, xin_count(*this))
                    if not (isinstance(t, int) and t < 2):
                        dve.wait_ge(y_stored[u], y_count(*last, u))
                    for i, (b, w0, w1) in enumerate(((6, 0, 4), (7, 4, WS))):
                        dve.wait_ge(proj_done, 2 * t + i + 1)
                        nc.vector.tensor_tensor(y_strip[u][:, w0:w1, :].rearrange("h w c -> h (w c)"), bk(b)[0:H, 0:C * (w1 - w0)],
                                                xres[:, w0:w1, :].rearrange("h w c -> h (w c)"), ALU.add).then_inc(y_done, 1)

                def normalise_out(t, m, b):
                    dve.wait_ge(av_done, 2 * t + m + 1)
                    av = bk(b)[0:PAIRP, 0:HP * NH * HV].rearrange("q (p h d) -> q p h d", p=HP, d=HV)
                    nc.vector.reciprocal(rc[m][0:PAIRP], av[:, :, :, HD]).then_inc(recip_done, 1)
                    dve.wait_ge(recip_done, 2 * t + m + 1)
                    nc.vector.tensor_tensor(o_norm[m][0:PAIRP], av[:, :, :, 0:HD],
                                            rc[m][0:PAIRP].unsqueeze(3).broadcast_to([PAIRP, HP, NH, HD]), ALU.mult).then_inc(on_done, 1)

                def step(n, j, u, prev, ahead):
                    t = n * NW + j
                    last = isinstance(j, int) and j == NW - 1
                    end_near = isinstance(j, int) and j == NW - 2
                    more = not (last and isinstance(n, int) and n == NI - 1)
                    kind = max(0, j - (NW - 3)) if isinstance(j, int) else 0
                    for i in range(NCH):
                        add_bias(t, i, kind)
                        row_max(t, i)
                        if prev and i == 0:
                            normalise_out(t - 1, 1, 7)
                    dve.wait_ge(v_done, t + 1)
                    src = bank3[PAD:PAIRP, :, 0:HP * C].rearrange("k b (p c) -> k b p c", c=C)
                    odd = v01[:, :, :].rearrange("k (b p a) c -> k a b p c", b=2, a=2)
                    nc.vector.tensor_copy(odd[0:TOK, 1, :, :, 0:HD], src[:, :, :, 0:HD]).then_inc(v_evac_dve, 1)
                    nc.vector.tensor_copy(odd[PAD:PAIRP, 1, :, :, HV:HV + HD], src[:, :, :, HD:2 * HD]).then_inc(v_evac_dve, 1)
                    src2 = bank3[PAD:PAIRP, :, 0:HP * C].rearrange("k b (g o c) -> k o b g c", o=2, c=C)
                    dst2 = v2[:, :, :, :, :].rearrange("k (b g) a o c -> k a o b g c", b=2)
                    nc.vector.tensor_copy(dst2[0:TOK, 1, 0, :, :, 0:HD], src2[:, 0, :, :, 2 * HD:C]).then_inc(v_evac_dve, 1)
                    nc.vector.tensor_copy(dst2[PAD:PAIRP, 1, 1, :, :, 0:HD], src2[:, 1, :, :, 2 * HD:C]).then_inc(v_evac_dve, 1)
                    if prev:
                        residual(t - 1, 1 - u, *before(n, j))
                    if ahead:
                        dve.wait_ge(xn_done, 2 * (t + 2))
                        move_xT(t + NW + 1, ahead_of(n, j)[1])
                    if more:
                        move_queries(t + 1)
                    if end_near:
                        if ahead:
                            x_statistics(t + NW + 1, NW - 1)
                        channel_statistics(n + 1, (n + 2) * NW, ahead)
                    if more:
                        move_keys(t + 1)
                    if end_near:
                        channel_spread(n + 1)
                    normalise_out(t, 0, 7)
                    if ahead and not end_near:
                        x_statistics(t + NW + 1, ahead_of(n, j)[1])
                    if end_near:
                        group_variance(n + 1)
                    if prev:
                        y_statistics(t - 1, j)
                    if end_near:
                        scale_and_shift(n + 1)
                        broadcast_y_statistics(n + 1)
                    if last:
                        keep_y_statistics(n + 1, t)

                def before(n, j):
                    if isinstance(j, int) and j == 0:
                        return (n - 1, NW - 3), (n - 1, NW - 1)
                    return (n, j - 3), (n, j - 1)

                move_queries(0)
                move_keys(0)
                walk(dve, step)
                normalise_out(NI * NW - 1, 1, 7)
                residual(NI * NW - 1, 1, *before(NI, 0))
                y_statistics(NI * NW - 1, 0)
                dve.wait_ge(y_stats, 2 * NI * NW)
                all_statistics(NI + 1, None, NI * NW, False)

            @block.tensor
            def _(pe):
                pe.wait_ge(psum_ready, 8)
                pe.wait_ge(consts_in, 16 * 14)
                nc.tensor.matmul(bk(7)[C:C + 1, 0:C], b_qkv[:, 2:3], w_proj[0:C, :], start=True, stop=True).then_inc(setup_mm, 1)

                def transposes(strip, done):
                    for w in range(WS):
                        b, at = (3, w) if w < 4 else (4, w - 4)
                        mm = nc.tensor.transpose(bk(b)[0:C, H * at:H * at + H], strip[:, w, :], ident[0:H, 0:H])
                        if w in (3, WS - 1):
                            mm.then_inc(done, 1)

                def transpose_x(n, j):
                    pe.wait_ge(xin_loaded, xin_ahead(n, j))
                    transposes(xin, xT_done)

                def transpose_first(u, dmas):
                    pe.wait_ge(first_loaded[u], 16 * dmas)
                    transposes(first_in[u], xT_done)

                def queries(t):
                    for i in range(2):
                        pe.wait_ge(xn_done, 2 * t + i + 1)
                        nc.tensor.matmul(q_bank(i)[0:QK0, 0:HS], w_qkv[:, 0:QK0], xn[:, NP * i:NP * i + NP, 0:TOK],
                                         start=True, stop=True).then_inc(qk_done, 1)

                def keys(s=None):
                    for i in range(2):
                        if s is not None:
                            pe.wait_ge((xT_evac_act, xT_evac_dve)[i], s + 1)
                        low = PAD if i else 0
                        nc.tensor.matmul(bk(3 + i)[low:low + C - HD, 0:HS], w_qkv[:, QK0:2 * C], xn[:, NP * i:NP * i + NP, 0:TOK],
                                         start=True, stop=True).then_inc(qk_done, 1)

                def scores(i):
                    p0, p1 = CHUNKS[i]
                    for w in range(2 * p0, 2 * p1):
                        a, at = w % 2, NH * TOK * (w // 2 - p0)
                        mm = nc.tensor.matmul(ps_scores[PAD * a:PAD * a + TOK, i, at:at + NH * TOK],
                                              q_sb[:, TOK * w:TOK * w + TOK],
                                              k_sb[:, w, :, :].rearrange("c h k -> c (h k)"), start=True, stop=True)
                    mm.then_inc(scores_done, 1)

                def values():
                    for p in range(NP):
                        mm = nc.tensor.matmul(bank3[0:PAIRP, p // HP, C * (p % HP):C * (p % HP) + C],
                                              xn[:, 2 * p:2 * p + 2, :].rearrange("c a k -> c (a k)")[:, 0:PAIRP],
                                              w_qkv[:, 2 * C:3 * C], start=True, stop=True)
                    mm.then_inc(v_done, 1)

                def transpose_p(m, first=0, end=HP):
                    for p in range(first, end):
                        mm = nc.tensor.transpose(bk(5)[0:PAIRP, 128 * p:128 * p + PAIRP],
                                                 p01[0:PAIRP, HP * m + p, :, :].rearrange("q a k -> q (a k)")[:, 0:PAIRP], ident[0:PAIRP, 0:PAIRP])
                    if end == HP:
                        mm.then_inc(pt_done, 1)

                def transpose_p2(m):
                    for g in range(HP // 2):
                        mm = nc.tensor.transpose(bk(6)[0:PAIRP, 128 * g:128 * g + PAIRP],
                                                 p2[0:PAIRP, HP * m + 2 * g:HP * m + 2 * g + 2, :].rearrange("q a k -> q (a k)")[:, 0:PAIRP], ident[0:PAIRP, 0:PAIRP])
                    mm.then_inc(pt_done, 1)

                def weighted_values(m, b):
                    av = bk(b)[:, 0:HP * NH * HV].rearrange("q (p d) -> q p d", p=HP)
                    for p in range(HP):
                        for a in range(2):
                            w = 2 * (HP * m + p) + a
                            rows = slice(PAD * a, PAD * a + TOK)
                            mm = nc.tensor.matmul(av[rows, p, 0:2 * HV], pt01[0:PAIRP, p, a, :], v01[0:PAIRP, w, :], start=True, stop=True)
                            if p % 2:
                                mm = nc.tensor.matmul(av[rows, p - 1:p + 1, 2 * HV:3 * HV], pt2[0:PAIRP, p // 2, a, :],
                                                      v2[0:PAIRP, (HP * m + p) // 2, a, :, :].rearrange("k o c -> k (o c)"), start=True, stop=True)
                    mm.then_inc(av_done, 1)

                def transpose_o(m, b):
                    for p in range(HP):
                        mm = nc.tensor.transpose(bk(b)[0:C, 128 * p:128 * p + PAIRP],
                                                 o_norm[m][0:PAIRP, p, :, :].rearrange("q h d -> q (h d)"), ident[0:PAIRP, 0:PAIRP])
                    mm.then_inc(ot_done, 1)

                def project():
                    for w in range(WS):
                        b, at = (6, w) if w < 4 else (7, w - 4)
                        mm = nc.tensor.matmul(bk(b)[0:H, C * at:C * at + C], oT[:, w, :, :].rearrange("c i h -> c (i h)"), w_proj[:, :], start=True, stop=True)
                        if w in (3, WS - 1):
                            mm.then_inc(proj_done, 1)

                def group_means(i):
                    pe.wait_ge(agg_dve, 3 * i + 1)
                    nc.tensor.matmul(ps_scores[0:C, 0, 500:502], group_sb[:, :], mv[:, :, 0], start=True, stop=True).then_inc(agg_pe, 1)

                def group_spreads(i):
                    pe.wait_ge(agg_dve, 3 * i + 2)
                    nc.tensor.matmul(ps_scores[0:C, 0, 504:506], group_sb[:, :], spread[:, :], start=True, stop=True).then_inc(agg_pe, 1)

                def row_forms(i):
                    pe.wait_ge(agg_copy, 7 * i + 6)
                    for s in range(3):
                        mm = nc.tensor.matmul(ps_scores[:, 0, C * s:C * s + C], stat_bc[:, s, :], ident[0:C, 0:C], start=True, stop=True)
                    mm.then_inc(rows_mm, 1)

                cuts = len(ROW_CUTS)
                transpose_first(0, cuts)
                for u in (1, 2):
                    pe.wait_ge(xT_evac_act, u)
                    pe.wait_ge(xT_evac_dve, u)
                    transpose_first(u, cuts)
                with pe.Fori(1, NW // 3) as k:
                    for u in range(3):
                        pe.wait_ge(xT_evac_act, 3 * k + u)
                        pe.wait_ge(xT_evac_dve, 3 * k + u)
                        transpose_first(u, cuts * (k + 1))
                pe.wait_ge(xT_evac_act, NW - 1)
                pe.wait_ge(xT_evac_dve, NW - 1)
                transpose_first(0, cuts * (NW // 3 + 2))
                pe.wait_ge(xT_evac_act, NW)
                pe.wait_ge(xT_evac_dve, NW)
                group_means(0)
                group_spreads(0)
                pe.wait_ge(consts_ready, 2)
                pe.wait_ge(setup_pool, 15)
                transpose_first(1, cuts * (NW // 3 + 1))
                queries(0)
                keys(NW)

                def step(n, j, u, prev, ahead):
                    t = n * NW + j
                    last = isinstance(j, int) and j == NW - 1
                    end_near = isinstance(j, int) and j == NW - 2
                    more = not (last and isinstance(n, int) and n == NI - 1)
                    s = t + NW + 1
                    pe.wait_ge(q_evac, 2 * t + 1)
                    pe.wait_ge(k_evac_act, 4 * t + 3)
                    pe.wait_ge(k_evac_dve, len(DVE_KEYS) * (2 * t + 1))
                    if prev:
                        pe.wait_ge(bias_added, NCH * t)
                    if prev and isinstance(j, int) and j == 0:
                        pe.wait_ge(rows_evac, n)
                    scores(0)
                    if prev:
                        pe.wait_ge(pt_evac, 4 * t)
                        pe.wait_ge(ot_evac, 2 * t - 1)
                        weighted_values(1, 7)
                    pe.wait_ge(q_evac, 2 * (t + 1))
                    pe.wait_ge(k_evac_act, 2 * len(ACT_KEYS) * (t + 1))
                    pe.wait_ge(k_evac_dve, 2 * len(DVE_KEYS) * (t + 1))
                    scores(1)
                    scores(2)
                    if prev:
                        pe.wait_ge(on_done, 2 * t)
                        transpose_o(1, 5)
                    if prev and not (isinstance(t, int) and t == 1):
                        pe.wait_ge(y_stats, 2 * (t - 1))
                    values()
                    if prev:
                        pe.wait_ge(ot_evac, 2 * t)
                        project()
                    pe.wait_ge(exp_done, 2 * NCH * t + 1)
                    transpose_p(0, 0, PB)
                    pe.wait_ge(v_evac_act, 4 * (t + 1))
                    pe.wait_ge(v_evac_dve, 4 * (t + 1))
                    if ahead:
                        transpose_x(*ahead_of(n, j))
                    if prev:
                        pe.wait_ge(y_done, 2 * t)
                    pe.wait_ge(exp_done, 2 * NCH * t + 4)
                    transpose_p(0, PB)
                    transpose_p2(0)
                    pe.wait_ge(bias_added, NCH * (t + 1))
                    if last:
                        row_forms(n + 1)
                    if more:
                        queries(t + 1)
                        keys(s if ahead else None)
                    pe.wait_ge(pt_evac, 4 * t + 2)
                    weighted_values(0, 7)
                    if end_near:
                        group_means(n + 1)
                    pe.wait_ge(exp_done, 2 * NCH * (t + 1))
                    transpose_p(1)
                    transpose_p2(1)
                    if end_near:
                        group_spreads(n + 1)
                    if more:
                        pe.wait_ge(k_evac_act, 2 * len(ACT_KEYS) * (t + 2))
                        pe.wait_ge(k_evac_dve, 2 * len(DVE_KEYS) * (t + 2))
                    if prev:
                        transposes(y_strip[1 - u], yT_done)
                    pe.wait_ge(on_done, 2 * t + 1)
                    transpose_o(0, 7)
                    if end_near:
                        pe.wait_ge(agg_dve, 3 * (n + 2))

                walk(pe, step)
                t = NI * NW
                pe.wait_ge(pt_evac, 4 * t)
                pe.wait_ge(ot_evac, 2 * t - 1)
                weighted_values(1, 7)
                pe.wait_ge(on_done, 2 * t)
                transpose_o(1, 5)
                pe.wait_ge(ot_evac, 2 * t)
                project()
                pe.wait_ge(y_done, 2 * t)
                transposes(y_strip[1], yT_done)
                pe.wait_ge(rows_evac, NI)
                group_means(NI + 1)
                group_spreads(NI + 1)
                row_forms(NI + 1)

        phase_c = ExitStack()
        with phase_c:
            band = phase_c.enter_context(nc.sbuf_tensor("band", [128, 2, C, 128], F32))
            y_img = [phase_c.enter_context(nc.sbuf_tensor(f"y_img{u}", [128, BLK * C], F32)) for u in range(2)]
            rows = [phase_c.enter_context(nc.sbuf_tensor(f"rows{u}", [128, 3, C], F32)) for u in range(2)]
            z = [phase_c.enter_context(nc.sbuf_tensor(f"z{u}", [128, CG, BLK], F32)) for u in range(3)]
            v = [phase_c.enter_context(nc.sbuf_tensor(f"gated_z{u}", [128, CG, OUTB], F32)) for u in range(3)]

            POOL_ADDS = [g for g in range(NCG) if g % 3]
            DVE_ADDS = [g for g in range(NCG) if g % 3 == 0]
            HALVES = ((slice(64, 128), 0), (slice(0, 64), NWB))
            MC = 64
            BANKS = 4

            def conv_bank(g):
                return (bk(3), bk(4), bk(5), bk(6))[g % BANKS]

            block = phase_c.enter_context(nc.Block())

            @block.sync
            def _(sp):
                for i in range(4):
                    if i >= 2:
                        sp.wait_ge(band_copied[i % 2], i // 2)
                    sp.dma_start(y_img[i % 2][:, 0:MC * C],
                                 band_dram[i // 2, :, MC * (i % 2):MC * (i % 2) + MC, :].rearrange("p m c -> p (m c)")
                                 ).then_inc(band_in[i % 2], 16)

                def load_rows(n, u):
                    sp.dma_start(rows[u][:, :, :].rearrange("p s c -> p (s c)"),
                                 rows_dram[bass.ds(n + 1, 1), :, :].rearrange("a p c -> (a p) c")).then_inc(y_in[u], 16)

                def load(n, u, r):
                    sp.dma_start(y_img[u][PC * r:PC * r + PC, :],
                                 y_patch[bass.ds(n + 1, 1), r, :, :, :, :].rearrange("a w b v c -> (a w) (b v c)")
                                 ).then_inc(y_in[u], 16)

                def store(n, u, r):
                    img = y_img[u][:, :].rearrange("p (b w c) -> p b w c", w=NWB, c=C)
                    row = (r + PR - HALO) % PR
                    b0 = 0 if r >= HALO else 1
                    for wb in range(NWB):
                        sp.dma_start(out[bass.ds(n, 1), row::PR, OC * wb:OC * wb + OC, :].rearrange("a b w c -> w (a b) c"),
                                     img[PC * r + HALO:PC * r + HALO + OC, b0:b0 + NB, wb, :]).then_inc(out_stored[r], 16)

                sp.wait_ge(y_stored[0], y_count(NI - 1, NW - 2, 0))
                sp.wait_ge(y_stored[1], y_count(NI - 1, NW - 1, 1))
                sp.wait_ge(rows_stored, 16 * BORDER * (NI + 1))
                for u in range(2):
                    sp.wait_ge(band_copied[u], 2)
                    load_rows(u, u)
                    for r in range(PR):
                        load(u, u, r)

                def finish(n, u):
                    sp.wait_ge(added_dve, 1 + len(DVE_ADDS) * 2 * (n + 1))
                    sp.wait_ge(added_pool, 2 + len(POOL_ADDS) * 2 * (n + 1))
                    for r in range(PR):
                        store(n, u, r)

                with sp.Fori(0, NI // 2 - 1) as k:
                    for u in range(2):
                        n = 2 * k + u
                        finish(n, u)
                        load_rows(n + 2, u)
                        for r in range(PR):
                            sp.wait_ge(out_stored[r], 16 * NWB * (n + 1))
                            load(n + 2, u, r)
                for u in range(2):
                    finish(NI - 2 + u, u)
                for r in range(PR):
                    sp.wait_ge(out_stored[r], 16 * NWB * NI)

            @block.scalar
            def _(act):
                for i in (0, 2):
                    act.wait_ge(band_in[0], 16 * (i // 2 + 1))
                    nc.scalar.activation(band[:, i // 2, :, 0:MC], y_img[0][:, 0:MC * C].rearrange("p (m c) -> p c m", c=C),
                                         ACT.Copy, scale=alpha_col).then_inc(band_copied[0], 1)

                def step(n, u):
                    act.wait_ge(y_in[u], 16 * (1 + PR) * (k_of(n, u) + 1))
                    img = y_img[u][:, :].rearrange("p (b c) -> p c b", c=C)
                    for g in range(NCG):
                        act.wait_ge(gated, 2 * BANKS + 2 * (NCG * n + g - 2))
                        for i in range(CG):
                            c = CG * g + i
                            zz = nc.scalar.activation(z[g % 3][:, i, :], img[:, c, :], ACT.Identity,
                                                      bias=rows[u][:, 2, c:c + 1], scale=rows[u][:, 1, c:c + 1])
                        zz.then_inc(z_ready, 1)

                with act.Fori(0, NI // 2) as k:
                    def k_of(n, u):
                        return k
                    for u in range(2):
                        step(2 * k + u, u)

            @block.tensor
            def _(pe):
                pe.wait_ge(band_copied[0], 2)
                pe.wait_ge(band_copied[1], 2)
                with pe.Fori(0, NI // 2) as k:
                    for u in range(2):
                        n = 2 * k + u
                        for g in range(NCG):
                            pe.wait_ge(z_ready, NCG * n + g + 1)
                            pe.wait_ge(gated, 2 * (NCG * n + g) + 2)
                            for i in range(CG):
                                o = conv_bank(g)[:, OUTB * i:OUTB * i + OUTB]
                                nc.tensor.matmul(o, band[:, 0, CG * g + i, :], z[g % 3][:, i, 0:OUTB], start=True, stop=False)
                                mm = nc.tensor.matmul(o, band[:, 1, CG * g + i, :], z[g % 3][:, i, NWB:NWB + OUTB], start=False, stop=True)
                            mm.then_inc(conv_done, 1)

            def add_group(engine, u, g, done):
                img = y_img[u][:, :].rearrange("p (b c) -> p c b", c=C)
                for rows_, b0 in HALVES:
                    part = img[rows_, CG * g:CG * g + CG, b0:b0 + OUTB]
                    engine.tensor_tensor(part, v[g % 3][rows_, :, :], part, ALU.add).then_inc(done, 1)

            @block.vector
            def _(dve):
                for i in (1, 3):
                    dve.wait_ge(band_in[1], 16 * (i // 2 + 1))
                    nc.vector.tensor_scalar(band[:, i // 2, :, MC:2 * MC], y_img[1][:, 0:MC * C].rearrange("p (m c) -> p c m", c=C),
                                            alpha_col, None, ALU.mult).then_inc(band_copied[1], 1)
                nc.vector.memset(v[0][:, :, :], 0.0).then_inc(added_dve, 1)
                for g in range(BANKS):
                    nc.vector.memset(conv_bank(g)[:, :], 0.0).then_inc(gated, 2)
                with dve.Fori(0, NI // 2) as k:
                    for u in range(2):
                        n = 2 * k + u
                        for g in range(NCG):
                            dve.wait_ge(conv_done, NCG * n + g + 1)
                            if g % 3:
                                dve.wait_ge(added_pool, 2 + 2 * (len(POOL_ADDS) * n + len([q for q in POOL_ADDS if q <= g - 3])))
                            else:
                                dve.wait_ge(added_dve, 1 + 2 * (len(DVE_ADDS) * n + len([q for q in DVE_ADDS if q <= g - 3])))
                            for rows_, b0 in HALVES:
                                nc.vector.scalar_tensor_tensor(
                                    v[g % 3][rows_, :, :], conv_bank(g)[rows_, 0:CG * OUTB].rearrange("p (c b) -> p c b", c=CG),
                                    gate_one[rows_, :], z[g % 3][rows_, :, b0:b0 + OUTB], ALU.add, ALU.mult).then_inc(gated, 1)
                            if g - 1 in DVE_ADDS:
                                dve.wait_ge(gated, 2 * BANKS + 2 * (NCG * n + g))
                                add_group(nc.vector, u, g - 1, added_dve)

            @block.gpsimd
            def _(pool):
                for q in (1, 2):
                    nc.gpsimd.memset(v[q][:, :, :], 0.0).then_inc(added_pool, 1)
                with pool.Fori(0, NI // 2) as k:
                    for u in range(2):
                        n = 2 * k + u
                        for g in POOL_ADDS:
                            pool.wait_ge(gated, 2 * BANKS + 2 * (NCG * n + g + 1))
                            add_group(nc.gpsimd, u, g, added_pool)


def host_bias_windows(table):
    import numpy as np
    flipped = table.reshape(2 * WS - 1, 2 * WS - 1, NH)[::-1, ::-1]
    last = WS - 1
    win = [flipped[last - h:last - h + WS, last - w:last - w + WS].transpose(2, 1, 0).reshape(NH, TOK)
           for w in range(WS) for h in range(WS)]
    return np.stack(win)


def host_masks():
    import numpy as np
    side = np.repeat([0, 1, 2], [H - WS, WS - SS, SS])
    side = np.roll(side, -SS).reshape(NW, WS)
    m = np.zeros((PAIRP, 3, 2, TOK), np.float32)
    for k, column in enumerate((0, NW - 2, NW - 1)):
        for i, (upper, lower) in enumerate(((0, 1), (NW - 2, NW - 1))):
            for start, row in ((0, upper), (PAD, lower)):
                region = (side[column][:, None] + 3 * side[row][None, :]).reshape(TOK)
                m[start:start + TOK, k, i] = np.where(region[:, None] != region[None, :], np.float32(-1e9), np.float32(0))
    return m


def kernel(x, L0_conv_qkv_w, L0_conv_qkv_b, L0_conv_proj_w, L0_conv_proj_b, L0_conv_bias_table,
           L1_conv_kernel, L1_conv_alpha, L1_conv_bias):
    import numpy as np
    import concourse.bacc as bacc
    from concourse.bass_utils import run_bass_kernel_spmd

    nc = bacc.Bacc("TRN2", target_bir_lowering=False, num_devices=1)
    arrays = {
        "x": x,
        "qkv_w": L0_conv_qkv_w,
        "qkv_b": np.asarray(L0_conv_qkv_b).reshape(3, C).T,
        "proj_w": L0_conv_proj_w,
        "proj_b": np.asarray(L0_conv_proj_b).reshape(1, C),
        "bias_win": host_bias_windows(np.asarray(L0_conv_bias_table)),
        "taps": L1_conv_kernel,
        "alpha": L1_conv_alpha,
        "bias": L1_conv_bias,
        "masks": host_masks(),
        "eye": np.eye(128, dtype=np.float32),
        "group": np.kron(np.eye(C // 3, dtype=np.float32), np.full((3, 3), 1 / 3, np.float32)),
    }
    arrays = {f"in_{k}": np.ascontiguousarray(a) for k, a in arrays.items()}
    aps = [nc.dram_tensor(k, a.shape, F32, kind="ExternalInput").ap() for k, a in arrays.items()]
    out = nc.dram_tensor("out", (NI, H, W, C), F32, kind="ExternalOutput").ap()
    attention_then_conv(nc, *aps, out)
    return run_bass_kernel_spmd(nc, [arrays], core_ids=[0]).results[0]["out"]
```
